# Optimizing a Trainium2 kernel written in Bass

```python
import numpy as np
import jax
import jax.numpy as jnp

def _softmax(x, axis=-1):
    return jax.nn.softmax(x, axis=axis)

def _gelu(x):
    return jax.nn.gelu(x, approximate=True)

def _silu(x):
    return jax.nn.silu(x)

def _sigmoid(x):
    return jax.nn.sigmoid(x)

def _layernorm(x, axis=-1, eps=1e-05):
    m = jnp.mean(x, axis=axis, keepdims=True)
    v = jnp.var(x, axis=axis, keepdims=True)
    return (x - m) / jnp.sqrt(v + eps)

def _scatter_add(tgt, idx, src, axis=0):
    return tgt.at[idx].add(src)

def _segment_sum(src, seg, n):
    return jax.ops.segment_sum(src, seg, n)
kernel_name = 'mk_flamingo_gated_d2_seqx_r8_c5c51d'

def setup_inputs(seed: int=0):
    np.random.seed(seed)
    _w = jnp.asarray

    def _rec_inputs():
        import jax
        import jax.numpy as jnp
        _rk = jax.random.key(seed)
        x = 7.22e-05 + 1 * jax.random.normal(jax.random.fold_in(_rk, 1), (128, 64, 128), jnp.float32)
        _lenS = 64 - jax.random.randint(jax.random.fold_in(_rk, 7), (128,), 0, max(1, 64 // 4) + 1, jnp.int32)
        _lenS2 = 64 - jax.random.randint(jax.random.fold_in(_rk, 8), (128,), 0, max(1, 64 // 4) + 1, jnp.int32)
        _ctx_1024P = jax.random.normal(jax.random.fold_in(_rk, 11), (128, 16, 128), jnp.float32)
        _ctx_1024c = jax.random.dirichlet(jax.random.fold_in(_rk, 511), 0.3 * jnp.ones((16,), jnp.float32), (128, 64))
        _ctx_1024t = jnp.einsum('bsk,bkd->bsd', _ctx_1024c, _ctx_1024P)
        _ctx_1024t = _ctx_1024t * jax.lax.rsqrt(jnp.mean(jnp.square(_ctx_1024t)) + 1e-12) * 0.953939
        ctx_1024 = 4.13588e-05 + 0.999923 * (_ctx_1024t + 0.3 * jax.random.normal(jax.random.fold_in(_rk, 611), (128, 64, 128), jnp.float32))
        _validS = jnp.arange(64)[None, :] < _lenS[:, None]
        _validS2 = jnp.arange(64)[None, :] < _lenS2[:, None]
        _causal = jnp.tril(jnp.ones((64, 64), dtype=bool))
        mask_1x1xSxS2_ik0 = jnp.where(jnp.broadcast_to(_validS2[0:1, None, None, :], (1, 1, 64, 64)), 0, 1).astype(jnp.int32)
        _g = jax.random.normal(jax.random.fold_in(_rk, 9001), (2, 2), jnp.float32)
        _g = jnp.sign(_g) * jnp.maximum(jnp.abs(_g), 1.0) + (_g == 0) * 1.0
        g_xattn = _g[0]
        g_ffn = _g[1]
        return (x, ctx_1024, mask_1x1xSxS2_ik0, g_xattn, g_ffn)
    x, ctx_1024, mask_1x1xSxS2_ik0, g_xattn, g_ffn = _rec_inputs()

    def _L0_xattn_setup():
        import jax, jax.numpy as jnp
        import numpy as np
        EMBED = 128
        HEADS = 16
        HEAD_DIM = EMBED // HEADS
        key = jax.random.key(seed)
        ks = jax.random.split(key, 11)
        B, S, D = (4, 256, EMBED)
        scale = 1.0 / np.sqrt(D)
        inp = {'query': jax.random.normal(ks[0], (B, S, D), dtype=jnp.float32), 'key': jax.random.normal(ks[1], (B, S, D), dtype=jnp.float32), 'value': jax.random.normal(ks[2], (B, S, D), dtype=jnp.float32), 'Wq': jax.random.normal(ks[3], (D, D), dtype=jnp.float32) * scale, 'bq': jnp.zeros((D,), dtype=jnp.float32), 'Wk': jax.random.normal(ks[4], (D, D), dtype=jnp.float32) * scale, 'bk': jnp.zeros((D,), dtype=jnp.float32), 'Wv': jax.random.normal(ks[5], (D, D), dtype=jnp.float32) * scale, 'bv': jnp.zeros((D,), dtype=jnp.float32), 'Wo': jax.random.normal(ks[6], (D, D), dtype=jnp.float32) * scale, 'bo': jnp.zeros((D,), dtype=jnp.float32)}
        return inp
    _L0_xattn_all = _L0_xattn_setup()
    _L0_xattn_in = {k: v for k, v in _L0_xattn_all.items() if k in ('Wq', 'bq', 'Wk', 'bk', 'Wv', 'bv', 'Wo', 'bo')}
    del _L0_xattn_all

    def _L0_ffn_setup():
        import jax, jax.numpy as jnp
        import numpy as np
        D_MODEL = 128
        E = 4
        MIN_E = 1
        TH_LO = 0.5
        TH_HI = 2.0
        key = jax.random.key(seed)
        ks = jax.random.split(key, 12)
        B, N, D, H = (4, 256, D_MODEL, 2 * D_MODEL)
        s = 0.02
        return {'x': jax.random.normal(ks[0], (B, N, D), dtype=jnp.float32), 'gate_w': jax.random.normal(ks[1], (D, E), dtype=jnp.float32) * s, 'gate_b': jnp.zeros((E,), dtype=jnp.float32), 'dp_w1': jax.random.normal(ks[2], (D, D // 2), dtype=jnp.float32) * s, 'dp_b1': jnp.zeros((D // 2,), dtype=jnp.float32), 'dp_w2': jax.random.normal(ks[3], (D // 2, 1), dtype=jnp.float32) * s, 'dp_b2': jnp.zeros((1,), dtype=jnp.float32), 'ew1': jax.random.normal(ks[4], (E, D, H), dtype=jnp.float32) * s, 'eb1': jnp.zeros((E, H), dtype=jnp.float32), 'ew2': jax.random.normal(ks[5], (E, H, D), dtype=jnp.float32) * s, 'eb2': jnp.zeros((E, D), dtype=jnp.float32)}
    _L0_ffn_all = _L0_ffn_setup()
    _L0_ffn_in = {k: v for k, v in _L0_ffn_all.items() if k in ('gate_w', 'gate_b', 'dp_w1', 'dp_b1', 'dp_w2', 'dp_b2', 'ew1', 'eb1', 'ew2', 'eb2')}
    del _L0_ffn_all

    def _L1_xattn_setup():
        import jax, jax.numpy as jnp
        import numpy as np
        EMBED = 128
        HEADS = 16
        HEAD_DIM = EMBED // HEADS
        B, S = (4, 256)
        key = jax.random.key(seed)
        ks = jax.random.split(key, 12)
        scale = 1.0 / np.sqrt(EMBED)
        inp = {'query': jax.random.normal(ks[0], (B, S, EMBED), jnp.float32), 'key_in': jax.random.normal(ks[1], (B, S, EMBED), jnp.float32), 'value': jax.random.normal(ks[2], (B, S, EMBED), jnp.float32), 'mask': jnp.tril(jnp.ones((S, S), jnp.int32))[None, None], 'Wq': jax.random.normal(ks[3], (EMBED, EMBED), jnp.float32) * scale, 'bq': jnp.zeros((EMBED,), jnp.float32), 'Wk': jax.random.normal(ks[4], (EMBED, EMBED), jnp.float32) * scale, 'bk': jnp.zeros((EMBED,), jnp.float32), 'Wv': jax.random.normal(ks[5], (EMBED, EMBED), jnp.float32) * scale, 'bv': jnp.zeros((EMBED,), jnp.float32), 'Wo': jax.random.normal(ks[6], (EMBED, EMBED), jnp.float32) * scale, 'bo': jnp.zeros((EMBED,), jnp.float32)}
        return inp
    _L1_xattn_all = _L1_xattn_setup()
    _L1_xattn_in = {k: v for k, v in _L1_xattn_all.items() if k in ('Wq', 'bq', 'Wk', 'bk', 'Wv', 'bv', 'Wo', 'bo')}
    del _L1_xattn_all

    def _L1_ffn_setup():
        import jax, jax.numpy as jnp
        import numpy as np
        B, S, D_MODEL, D_HIDDEN = (4, 256, 128, 512)

        def act_quant(x):
            scale = 127.0 / jnp.clip(jnp.max(jnp.abs(x), axis=-1, keepdims=True), 1e-05)
            return jnp.clip(jnp.round(x * scale), -128, 127) / scale

        def weight_quant(w):
            scale = 1.0 / jnp.clip(jnp.mean(jnp.abs(w)), 1e-05)
            return jnp.clip(jnp.round(w * scale), -1, 1) / scale

        def bit_linear(x, w):
            xq = x + jax.lax.stop_gradient(act_quant(x) - x)
            wq = w + jax.lax.stop_gradient(weight_quant(w) - w)
            return jnp.einsum('bsd,hd->bsh', xq, wq)

        def depthwise_conv1d(x_bcl, w, b):
            y = jax.lax.conv_general_dilated(x_bcl, w, window_strides=(1,), padding=[(1, 1)], dimension_numbers=('NCH', 'OIH', 'NCH'), feature_group_count=x_bcl.shape[1])
            return y + b[None, :, None]
        key = jax.random.key(seed)
        ks = jax.random.split(key, 5)
        lim1 = 1.0 / np.sqrt(D_MODEL)
        lim2 = 1.0 / np.sqrt(D_HIDDEN)
        limc = 1.0 / np.sqrt(3.0)
        return {'x': jax.random.normal(ks[0], (B, S, D_MODEL), dtype=jnp.float32), 'w1': jax.random.uniform(ks[1], (D_HIDDEN, D_MODEL), jnp.float32, -lim1, lim1), 'conv_w': jax.random.uniform(ks[2], (D_HIDDEN, 1, 3), jnp.float32, -limc, limc), 'conv_b': jax.random.uniform(ks[3], (D_HIDDEN,), jnp.float32, -limc, limc), 'w2': jax.random.uniform(ks[4], (D_MODEL, D_HIDDEN), jnp.float32, -lim2, lim2)}
    _L1_ffn_all = _L1_ffn_setup()
    _L1_ffn_in = {k: v for k, v in _L1_ffn_all.items() if k in ('w1', 'conv_w', 'conv_b', 'w2')}
    del _L1_ffn_all
    return {'x': x, 'ctx_1024': ctx_1024, 'mask_1x1xSxS2_ik0': mask_1x1xSxS2_ik0, 'g_xattn': g_xattn, 'g_ffn': g_ffn, 'L0_xattn_Wq': _L0_xattn_in['Wq'], 'L0_xattn_bq': _L0_xattn_in['bq'], 'L0_xattn_Wk': _L0_xattn_in['Wk'], 'L0_xattn_bk': _L0_xattn_in['bk'], 'L0_xattn_Wv': _L0_xattn_in['Wv'], 'L0_xattn_bv': _L0_xattn_in['bv'], 'L0_xattn_Wo': _L0_xattn_in['Wo'], 'L0_xattn_bo': _L0_xattn_in['bo'], 'L0_ffn_gate_w': _L0_ffn_in['gate_w'], 'L0_ffn_gate_b': _L0_ffn_in['gate_b'], 'L0_ffn_dp_w1': _L0_ffn_in['dp_w1'], 'L0_ffn_dp_b1': _L0_ffn_in['dp_b1'], 'L0_ffn_dp_w2': _L0_ffn_in['dp_w2'], 'L0_ffn_dp_b2': _L0_ffn_in['dp_b2'], 'L0_ffn_ew1': _L0_ffn_in['ew1'], 'L0_ffn_eb1': _L0_ffn_in['eb1'], 'L0_ffn_ew2': _L0_ffn_in['ew2'], 'L0_ffn_eb2': _L0_ffn_in['eb2'], 'L1_xattn_Wq': _L1_xattn_in['Wq'], 'L1_xattn_bq': _L1_xattn_in['bq'], 'L1_xattn_Wk': _L1_xattn_in['Wk'], 'L1_xattn_bk': _L1_xattn_in['bk'], 'L1_xattn_Wv': _L1_xattn_in['Wv'], 'L1_xattn_bv': _L1_xattn_in['bv'], 'L1_xattn_Wo': _L1_xattn_in['Wo'], 'L1_xattn_bo': _L1_xattn_in['bo'], 'L1_ffn_w1': _L1_ffn_in['w1'], 'L1_ffn_conv_w': _L1_ffn_in['conv_w'], 'L1_ffn_conv_b': _L1_ffn_in['conv_b'], 'L1_ffn_w2': _L1_ffn_in['w2']}

def reference(x, ctx_1024, mask_1x1xSxS2_ik0, g_xattn, g_ffn, L0_xattn_Wq, L0_xattn_bq, L0_xattn_Wk, L0_xattn_bk, L0_xattn_Wv, L0_xattn_bv, L0_xattn_Wo, L0_xattn_bo, L0_ffn_gate_w, L0_ffn_gate_b, L0_ffn_dp_w1, L0_ffn_dp_b1, L0_ffn_dp_w2, L0_ffn_dp_b2, L0_ffn_ew1, L0_ffn_eb1, L0_ffn_ew2, L0_ffn_eb2, L1_xattn_Wq, L1_xattn_bq, L1_xattn_Wk, L1_xattn_bk, L1_xattn_Wv, L1_xattn_bv, L1_xattn_Wo, L1_xattn_bo, L1_ffn_w1, L1_ffn_conv_w, L1_ffn_conv_b, L1_ffn_w2):
    import jax
    import jax.numpy as jnp

    def _L0_xattn_ref(query, key, value, Wq, bq, Wk, bk, Wv, bv, Wo, bo):
        import jax, jax.numpy as jnp
        import numpy as np
        EMBED = 128
        HEADS = 16
        HEAD_DIM = EMBED // HEADS
        B, S, D = query.shape
        H, Hd = (HEADS, HEAD_DIM)

        def split_heads(x):
            return x.reshape(B, -1, H, Hd).transpose(0, 2, 1, 3)
        q = split_heads(query @ Wq.T + bq)
        k = split_heads(key @ Wk.T + bk)
        v = split_heads(value @ Wv.T + bv)
        attn = jnp.einsum('bhsd,bhtd->bhst', q, k) / jnp.sqrt(jnp.float32(Hd))
        attn = jax.nn.softmax(attn, axis=-1)
        out = jnp.einsum('bhst,bhtd->bhsd', attn, v)
        out = out.transpose(0, 2, 1, 3).reshape(B, -1, D)
        return out @ Wo.T + bo

    def _L0_ffn_ref(x, gate_w, gate_b, dp_w1, dp_b1, dp_w2, dp_b2, ew1, eb1, ew2, eb2):
        import jax, jax.numpy as jnp
        import numpy as np
        D_MODEL = 128
        E = 4
        MIN_E = 1
        TH_LO = 0.5
        TH_HI = 2.0
        B, N, D = x.shape
        xf = x.reshape(B * N, D)
        T = B * N
        h = jax.nn.relu(xf @ dp_w1 + dp_b1)
        entropy = jax.nn.softplus(h @ dp_w2 + dp_b2)[:, 0]
        norm = jnp.clip((entropy - TH_LO) / (TH_HI - TH_LO), 0.0, 1.0)
        k_tok = jnp.clip(jnp.round(MIN_E + norm * (E - MIN_E)).astype(jnp.int32), MIN_E, E)
        logits = xf @ gate_w + gate_b
        top_logits, top_idx = jax.lax.top_k(logits, E)
        pos = jnp.arange(E)
        sel = pos[None, :] < k_tok[:, None]
        masked = jnp.where(sel, top_logits, -jnp.inf)
        w_top = jax.nn.softmax(masked, axis=-1)
        dense_w = jnp.zeros((T, E), dtype=xf.dtype).at[jnp.arange(T)[:, None], top_idx].set(w_top)
        hid = jax.nn.relu(jnp.einsum('td,edh->teh', xf, ew1) + eb1[None, :, :])
        y = jnp.einsum('teh,ehd->ted', hid, ew2) + eb2[None, :, :]
        out = jnp.einsum('te,ted->td', dense_w, y)
        return out.reshape(B, N, D)

    def _L1_xattn_ref(query, key_in, value, mask, Wq, bq, Wk, bk, Wv, bv, Wo, bo):
        import jax, jax.numpy as jnp
        import numpy as np
        EMBED = 128
        HEADS = 16
        HEAD_DIM = EMBED // HEADS
        B, S = (4, 256)
        b = query.shape[0]
        Q = query @ Wq.T + bq
        K = key_in @ Wk.T + bk
        V = value @ Wv.T + bv
        Q = Q.reshape(b, -1, HEADS, HEAD_DIM).transpose(0, 2, 1, 3)
        K = K.reshape(b, -1, HEADS, HEAD_DIM).transpose(0, 2, 1, 3)
        V = V.reshape(b, -1, HEADS, HEAD_DIM).transpose(0, 2, 1, 3)
        scores = jnp.einsum('bhqd,bhkd->bhqk', Q, K) / np.sqrt(HEAD_DIM)
        scores = jnp.where(mask == 0, jnp.float32(-1e+20), scores)
        probs = jax.nn.softmax(scores, axis=-1)
        attn = jnp.einsum('bhqk,bhkd->bhqd', probs, V)
        attn = attn.transpose(0, 2, 1, 3).reshape(b, -1, EMBED)
        return attn @ Wo.T + bo

    def _L1_ffn_ref(x, w1, conv_w, conv_b, w2):
        import jax, jax.numpy as jnp
        import numpy as np
        B, S, D_MODEL, D_HIDDEN = (4, 256, 128, 512)

        def act_quant(x):
            scale = 127.0 / jnp.clip(jnp.max(jnp.abs(x), axis=-1, keepdims=True), 1e-05)
            return jnp.clip(jnp.round(x * scale), -128, 127) / scale

        def weight_quant(w):
            scale = 1.0 / jnp.clip(jnp.mean(jnp.abs(w)), 1e-05)
            return jnp.clip(jnp.round(w * scale), -1, 1) / scale

        def bit_linear(x, w):
            xq = x + jax.lax.stop_gradient(act_quant(x) - x)
            wq = w + jax.lax.stop_gradient(weight_quant(w) - w)
            return jnp.einsum('bsd,hd->bsh', xq, wq)

        def depthwise_conv1d(x_bcl, w, b):
            y = jax.lax.conv_general_dilated(x_bcl, w, window_strides=(1,), padding=[(1, 1)], dimension_numbers=('NCH', 'OIH', 'NCH'), feature_group_count=x_bcl.shape[1])
            return y + b[None, :, None]
        h = bit_linear(x, w1)
        h = depthwise_conv1d(h.transpose(0, 2, 1), conv_w, conv_b)
        h = h.transpose(0, 2, 1)
        h = jax.nn.silu(h)
        return bit_linear(h, w2)
    x = x + jnp.tanh(g_xattn[0]) * _L0_xattn_ref(_layernorm(x, axis=-1), ctx_1024, ctx_1024, L0_xattn_Wq, L0_xattn_bq, L0_xattn_Wk, L0_xattn_bk, L0_xattn_Wv, L0_xattn_bv, L0_xattn_Wo, L0_xattn_bo)
    x = x + jnp.tanh(g_ffn[0]) * _L0_ffn_ref(_layernorm(x, axis=-1), L0_ffn_gate_w, L0_ffn_gate_b, L0_ffn_dp_w1, L0_ffn_dp_b1, L0_ffn_dp_w2, L0_ffn_dp_b2, L0_ffn_ew1, L0_ffn_eb1, L0_ffn_ew2, L0_ffn_eb2)
    x = x + jnp.tanh(g_xattn[1]) * _L1_xattn_ref(_layernorm(x, axis=-1), ctx_1024, ctx_1024, mask_1x1xSxS2_ik0, L1_xattn_Wq, L1_xattn_bq, L1_xattn_Wk, L1_xattn_bk, L1_xattn_Wv, L1_xattn_bv, L1_xattn_Wo, L1_xattn_bo)
    x = x + jnp.tanh(g_ffn[1]) * _L1_ffn_ref(_layernorm(x, axis=-1), L1_ffn_w1, L1_ffn_conv_w, L1_ffn_conv_b, L1_ffn_w2)
    return x

_drawn_inputs = setup_inputs


def setup_inputs(seed=0):
    import zlib

    import numpy as np

    out = dict(_drawn_inputs(seed))
    spreads = {'g_ffn': (-1.0, 0.6),
     'L0_xattn_bq': (0.0, 0.358),
     'L0_xattn_bk': (0.0, 0.8),
     'L0_xattn_bv': (0.0, 0.1),
     'L0_xattn_bo': (0.0, 0.1),
     'L0_ffn_gate_b': (0.0, 0.1),
     'L0_ffn_dp_b1': (0.0, 0.1),
     'L0_ffn_eb1': (0.0, 0.462),
     'L0_ffn_eb2': (0.0, 0.1),
     'L1_xattn_bq': (0.0, 0.305),
     'L1_xattn_bk': (0.0, 0.8),
     'L1_xattn_bv': (0.0, 0.1),
     'L1_xattn_bo': (0.0, 0.1)}
    factors = {}
    for name, (base, spread) in spreads.items():
        noise = np.random.default_rng([zlib.crc32(name.encode()), seed]).standard_normal(out[name].shape)
        drawn = base * np.exp(spread * noise) if base else spread * noise
        out[name] = jnp.asarray(drawn.astype(out[name].dtype))
    for name, factor in factors.items():
        out[name] = (out[name] * factor).astype(out[name].dtype)
    return out
```

```python
import math

import concourse.bass as bass
from concourse import mybir
from contextlib import ExitStack

F32 = mybir.dt.float32
BF16 = mybir.dt.bfloat16
I32 = mybir.dt.int32
ALU = mybir.AluOpType
ACT = mybir.ActivationFunctionType
AX = mybir.AxisListType

P = 128
B, S, D = 128, 64, 128
H, HD = 16, 8
BT = P // S
T = B // BT
NPAIR = H // 2
JH, RQ = 4, 4
E, HE = 4, 256
EC = E * HE // P
DPH = 64
GW = E + DPH
F = 512
FC = F // P
TAPS = 3
VW = HD + 1
LN_EPS = 1e-5
Q_EPS = 1e-5
SCALE = 1.0 / math.sqrt(HD)
NEG = 1e30
ROUND = 1.5 * 2.0 ** 23

C_ID, C_ONE, C_J, C_R, C_H, C_TIE, C_THR, C_POW, C_RND = 0, 128, 256, 260, 264, 266, 282, 285, 286
C_ALL = 287


def build(nc, a, out):
    with ExitStack() as ctx:
        def sb(name, shape, dt=F32):
            return ctx.enter_context(nc.sbuf_tensor(name, shape, dt))

        def sem(name):
            return ctx.enter_context(nc.semaphore(name))

        bank = [ctx.enter_context(nc.psum_tensor(f"bank{i}", [P, 512], F32)) for i in range(8)]

        const = sb("const", [P, C_ALL])
        ident = const[:, C_ID:C_ID + P]
        ones = const[:, C_ONE:C_ONE + P]
        ident16 = sb("ident16", [P, P], BF16)
        x_all = sb("x_all", [P, T * D])
        tg = sb("tg", [P, 4])
        graw = sb("graw", [P, 4])

        w_raw = sb("w_raw", [P, 2, 4, P])
        w_t = sb("w_t", [P, 2, 4, P])
        b_col = sb("b_col", [P, 2, 3])
        bo_row = sb("bo_row", [P, 2, P])
        q_mask = sb("q_mask", [P, 2, RQ, P])
        neg_mask = sb("neg_mask", [P, S], BF16)
        m_int = sb("m_int", [P, S], I32)
        m_keep = sb("m_keep", [P, S])
        m_any = sb("m_any", [P, 1])
        m_dead = sb("m_dead", [P, 1])
        m_keep2 = sb("m_keep2", [P, S])
        m_diag = sb("m_diag", [S, S])

        gate_w = sb("gate_w", [P, GW])
        gate_b = sb("gate_b", [P, GW])
        dp_w2 = sb("dp_w2", [P, DPH])
        dp_b2 = sb("dp_b2", [P, 1])
        thr = sb("thr", [P, E - 1])
        ew1 = sb("ew1", [P, EC, P])
        eb1 = sb("eb1", [P, EC])
        ew2 = sb("ew2", [P, EC, P])
        eb2 = sb("eb2", [P, E, P])

        f_w1 = sb("f_w1", [P, FC, D])
        f_w2 = sb("f_w2", [P, F])
        f_cw = sb("f_cw", [P, FC, TAPS])
        f_cb = sb("f_cb", [P, F])
        f_tap = sb("f_tap", [P, TAPS, FC, D])
        f_wk = sb("f_wk", [P, TAPS, F])
        f_w2t = sb("f_w2t", [P, FC, D], BF16)
        f_s = sb("f_s", [P, 8])

        ln_st = sb("ln_st", [P, 2, 6])
        ln_mv = sb("ln_mv", [P, 2, 5])
        ln_ve = sb("ln_ve", [P, 2, 1])
        ln_nm = sb("ln_nm", [P, 2, 1])
        ln_rs = sb("ln_rs", [P, 2, 1])
        ln_nr = sb("ln_nr", [P, 2, 1])
        xn = sb("xn", [P, 2, D])

        ctx_in = sb("ctx_in", [P, 2, D])
        xct = sb("xct", [P, 2, 2, BT, 2, S])
        qq = sb("qq", [P, 2, RQ, P])
        kj = sb("kj", [P, 2, JH, P])
        vb = sb("vb", [P, 2, NPAIR, BT, 2, VW])
        smax = sb("smax", [P, H])
        prob = sb("prob", [P, 2, H * S])
        prob_t = sb("prob_t", [P, NPAIR, P])
        rden = sb("rden", [P, H])
        o_n = sb("o_n", [P, 2, P])
        o_t = sb("o_t", [P, P])

        mxt = sb("mxt", [P, 2, P])
        hid = sb("hid", [P, 2, EC, P])
        gl = sb("gl", [P, GW])
        gj = sb("gj", [P, DPH])
        gz = sb("gz", [P, 1])
        gk = sb("gk", [P, 1])
        gs3 = sb("gs3", [P, E - 1])
        gm = sb("gm", [P, 1])
        ge = sb("ge", [P, E])
        g_gt = sb("g_gt", [P, E, E])
        g_eq = sb("g_eq", [P, E, E])
        g_rank = sb("g_rank", [P, E])
        g_ew = sb("g_ew", [P, E])
        g_sum = sb("g_sum", [P, 1])
        g_rs = sb("g_rs", [P, 1])
        gwt = sb("gwt", [P, 2, E])
        eb_t = sb("eb_t", [P, E, P])
        eb_acc = sb("eb_acc", [P, 2, P])
        y_acc = sb("y_acc", [P, 2, P])

        a1 = sb("a1", [P, 2, 4])
        a1i = sb("a1i", [P, 2, 1])
        q1 = sb("q1", [P, D])
        xdq = sb("xdq", [P, 2, D])
        xtap = sb("xtap", [P, 2, TAPS, BT, S])
        hpre = sb("hpre", [P, 2, F])
        hact = sb("hact", [P, 2, F])
        a2 = sb("a2", [P, 4])
        a2f = sb("a2f", [P, 2, 1])
        a2s = sb("a2s", [P, 2, 1])
        q2 = sb("q2", [P, 2, F])
        q2t = sb("q2t", [P, 2, F], BF16)

        names = """const_in attn_w_in moe_w_in ffn_w_in g_in mask_in
            tanh_done ident16_done w_tr w_copied setup_v mask_v alive_mm ones_set
            sum_mm ffn_sum tern tap_ready tap_tr tap_copied w2t_copied setup_act
            ln ln_ready xn_ready
            xc_tr xc_copied qkv_mm qk_ready v_ready scores_mm smax_done sub_done exp_done
            p_tr p_copied pv_mm rden_done o_norm o_tr o_copied wo_mm bo_added x_attn
            mx_tr mx_copied hid_mm gate_mm hid_v hid_a gate_v exp_gate gate_done eb_v eb_added y_mm y_v
            q1_v q1_ready q1_done xq_ready xq_tr xq_copied conv_mm hpre_done silu_done a2_v a2_ready q2_ready
            q2_tr q2_copied out_mm x_out""".split()
        s = {n: sem(n) for n in names}
        x_in = [sem(f"x_in{i}") for i in range(2)]
        ctx_ld = [sem(f"ctx_ld{i}") for i in range(2)]
        stored = sem("stored")

        def wait(eng, name, value):
            if isinstance(value, int) and value <= 0:
                return
            eng.wait_ge(s[name], value)

        def run_tiles(eng, step, lead, lag):
            lo = 2
            n = (T - lead - lo) // 2
            for t in range(-lead, lo):
                step(t, t % 2, lambda k: 0 <= t + k < T)
            with eng.Fori(0, n) as i:
                for par in range(2):
                    step(i * 2 + (lo + par), par, lambda k: True)
            for t in range(lo + 2 * n, T + lag):
                step(t, t % 2, lambda k: 0 <= t + k < T)

        LN_STEPS = 6

        def x_tile(t):
            return x_all[:, bass.ds(t * D, D)]

        def ln_stats(dve, f, t, par):
            n = f * T + t
            if f == 0:
                dve.wait_ge(x_in[par], (t + (2 - par)) * 8)
            else:
                wait(dve, (None, "x_attn", "y_v", "x_attn")[f], (0, t + 1, 4 * t + 4, T + t + 1)[f])
            wait(dve, "ln_ready", n - 1)
            wait(dve, "xn_ready", n - 1)
            dve.bn_stats(ln_st[:, par, :], x_tile(t)).then_inc(s["ln"], 1)
            dve.wait_ge(s["ln"], n * LN_STEPS + 1)
            even, odd = ln_st[:, par, 0:3], ln_st[:, par, 3:6]
            dve.tensor_tensor(ln_mv[:, par, 0:3], even, odd, ALU.add).then_inc(s["ln"], 1)
            dve.tensor_scalar(ln_mv[:, par, 3:4], even[:, 1:2], odd[:, 1:2], 0.5, ALU.subtract, ALU.mult)\
                .then_inc(s["ln"], 1)
            dve.wait_ge(s["ln"], n * LN_STEPS + 3)
            dve.tensor_scalar(ln_mv[:, par, 4:5], ln_mv[:, par, 2:3], 1.0 / D, LN_EPS, ALU.mult, ALU.add)\
                .then_inc(s["ln"], 1)
            dve.tensor_scalar(ln_nm[:, par, :], ln_mv[:, par, 1:2], -0.5, None, ALU.mult).then_inc(s["ln"], 1)
            dve.wait_ge(s["ln"], n * LN_STEPS + 5)
            dve.scalar_tensor_tensor(out=ln_ve[:, par, :], in0=ln_mv[:, par, 3:4], scalar=ln_mv[:, par, 3:4],
                                     in1=ln_mv[:, par, 4:5], op0=ALU.mult, op1=ALU.add).then_inc(s["ln"], 1)

        def ln_rstd(pool, f, t, par):
            n = f * T + t
            wait(pool, "ln", n * LN_STEPS + LN_STEPS)
            wait(pool, "xn_ready", n - 1)
            pool.tensor_tensor(ln_rs[:, par, :], ln_ve[:, par, :], const[:, C_POW:C_POW + 1], ALU.pow)\
                .then_inc(s["ln_ready"], 1)
            pool.wait_ge(s["ln_ready"], n * 2 + 1)
            pool.tensor_tensor(ln_nr[:, par, :], ln_nm[:, par, :], ln_rs[:, par, :], ALU.mult)\
                .then_inc(s["ln_ready"], 1)

        def ln_apply(act, f, t, par, free, free_at):
            n = f * T + t
            wait(act, "ln_ready", n * 2 + 2)
            wait(act, free, free_at)
            act.activation(xn[:, par, :], x_tile(t), ACT.Identity, bias=ln_nr[:, par, :],
                           scale=ln_rs[:, par, :]).then_inc(s["xn_ready"], 1)

        block = ctx.enter_context(nc.Block())

        @block.sync
        def _(sp):
            def load(dst, src, name):
                sp.dma_start(dst, src).then_inc(s[name], 16)

            def col(v):
                return v.rearrange("(p o) -> p o", o=1)

            load(const[:], a["const"], "const_in")
            for L in range(2):
                for n, w in enumerate("qkvo"):
                    load(w_raw[:, L, n, :], a[f"L{L}_xattn_W{w}"], "attn_w_in")
                for n, w in enumerate("qkv"):
                    load(b_col[:, L, n:n + 1], col(a[f"L{L}_xattn_b{w}"]), "attn_w_in")
                load(bo_row[:, L, :], a[f"L{L}_xattn_bo"].partition_broadcast(P), "attn_w_in")
            load(graw[:, 0:2], a["g_xattn"].partition_broadcast(P), "g_in")
            load(graw[:, 2:4], a["g_ffn"].partition_broadcast(P), "g_in")
            for b in range(BT):
                load(m_int[b * S:(b + 1) * S, :], a["mask_1x1xSxS2_ik0"][0, 0], "mask_in")

            x_d = a["x"].rearrange("b s d -> (b s) d")
            c_d = a["ctx_1024"].rearrange("b s d -> (b s) d")
            o_d = out.rearrange("b s d -> (b s) d")

            def load_ctx(L, t, par):
                wait(sp, "xc_tr", L * T + t - 1)
                sp.dma_start(ctx_in[:, par, :], c_d[bass.ds(t * P, P), :]).then_inc(ctx_ld[par], 16)

            def attention0(t, par, has):
                if has(3):
                    if not isinstance(t, int) or t + 3 >= 2:
                        wait(sp, "ln", (t + 2) * LN_STEPS)
                    sp.dma_start(x_all[:, bass.ds((t + 3) * D, D)], x_d[bass.ds((t + 3) * P, P), :])\
                        .then_inc(x_in[1 - par], 16)
                if has(1):
                    load_ctx(0, t + 1, 1 - par)

            run_tiles(sp, attention0, 3, 0)

            load(gate_w[:, 0:E], a["L0_ffn_gate_w"], "moe_w_in")
            load(gate_w[:, E:GW], a["L0_ffn_dp_w1"], "moe_w_in")
            load(gate_b[:, 0:E], a["L0_ffn_gate_b"].partition_broadcast(P), "moe_w_in")
            load(gate_b[:, E:GW], a["L0_ffn_dp_b1"].partition_broadcast(P), "moe_w_in")
            load(dp_w2[:], a["L0_ffn_dp_w2"].rearrange("h o -> (h o)").partition_broadcast(P), "moe_w_in")
            load(dp_b2[:], a["L0_ffn_dp_b2"].partition_broadcast(P), "moe_w_in")
            for e in range(E):
                load(ew1[:, e * 2:e * 2 + 2, :], a["L0_ffn_ew1"][e].rearrange("d (c h) -> d c h", c=2), "moe_w_in")
                load(ew2[:, e * 2:e * 2 + 2, :], a["L0_ffn_ew2"][e].rearrange("(c h) d -> h c d", c=2), "moe_w_in")
                load(eb2[:, e, :], a["L0_ffn_eb2"][e].partition_broadcast(P), "moe_w_in")
                for c in range(2):
                    load(eb1[:, e * 2 + c:e * 2 + c + 1], col(a["L0_ffn_eb1"][e, c * P:(c + 1) * P]), "moe_w_in")
            load(f_w1[:], a["L1_ffn_w1"].rearrange("(c p) d -> p c d", p=P), "ffn_w_in")
            load(f_w2[:], a["L1_ffn_w2"], "ffn_w_in")
            load(f_cw[:], a["L1_ffn_conv_w"].rearrange("(c p) o k -> p c (o k)", p=P), "ffn_w_in")
            load(f_cb[:], a["L1_ffn_conv_b"].partition_broadcast(P), "ffn_w_in")

            def attention1(t, par, has):
                if has(1):
                    load_ctx(1, t + 1, 1 - par)

            run_tiles(sp, attention1, 1, 0)

            def store(t, par, has):
                wait(sp, "x_out", t + 1)
                sp.dma_start(o_d[bass.ds(t * P, P), :], x_tile(t)).then_inc(stored, 16)

            run_tiles(sp, store, 0, 0)
            sp.wait_ge(stored, 16 * T)

        MOE_LOADS = 6 + E * 5

        @block.gpsimd
        def _(pool):
            pool.memset(xtap[:], 0.0).then_inc(s["ones_set"], 1)
            pool.wait_ge(s["const_in"], 16)

            def attention(L):
                def step(t, par, has):
                    if has(3):
                        ln_rstd(pool, 2 * L, t + 3, 1 - par)
                    if has(1):
                        n = L * T + t + 1
                        wait(pool, "xn_ready", 2 * L * T + t + 2)
                        pool.tensor_tensor(x_tile(t + 1), x_tile(t + 1), bo_row[:, L, :], ALU.add)\
                            .then_inc(s["bo_added"], 1)
                return step

            pool.wait_ge(s["setup_v"], 2)
            run_tiles(pool, attention(0), 3, 0)

            def experts(t, par, has):
                if has(3):
                    ln_rstd(pool, 1, t + 3, 1 - par)
                if has(0):
                    wait(pool, "gate_done", t + 1)
                    wait(pool, "eb_added", t)
                    pool.tensor_tensor(eb_t[:, 0, :], eb2[:, 0, :], gwt[:, par, 0:1].to_broadcast([P, P]), ALU.mult)\
                        .then_inc(s["eb_v"], 1)
                    for e in range(1, E):
                        pool.tensor_scalar(eb_t[:, e, :], eb2[:, e, :], gwt[:, par, e:e + 1], 0.0, ALU.mult, ALU.add)\
                            .then_inc(s["eb_v"], 1)
                    pool.wait_ge(s["eb_v"], t * 6 + 4)
                    pool.tensor_tensor(eb_acc[:, :, :], eb_t[:, 0:2, :], eb_t[:, 2:4, :], ALU.add).then_inc(s["eb_v"], 1)
                    pool.wait_ge(s["eb_v"], t * 6 + 5)
                    pool.tensor_tensor(eb_t[:, 0, :], eb_acc[:, 0, :], eb_acc[:, 1, :], ALU.add).then_inc(s["eb_v"], 1)
                    pool.wait_ge(s["eb_v"], t * 6 + 6)
                    wait(pool, "xn_ready", T + t + 1)
                    pool.tensor_tensor(x_tile(t), x_tile(t), eb_t[:, 0, :], ALU.add).then_inc(s["eb_added"], 1)

            run_tiles(pool, experts, 3, 0)
            run_tiles(pool, attention(1), 3, 0)

            def ffn(t, par, has):
                if has(3):
                    ln_rstd(pool, 3, t + 3, 1 - par)

            run_tiles(pool, ffn, 3, 0)

        @block.scalar
        def _(act):
            act.wait_ge(s["g_in"], 32)
            act.activation(tg[:], graw[:], ACT.Tanh).then_inc(s["tanh_done"], 1)
            act.wait_ge(s["tanh_done"], 1)
            for L in range(2):
                act.wait_ge(s["w_tr"], L + 1)
                act.activation(w_t[:, L, 0:3, :], bank[L][:, 0:3 * P], ACT.Copy).then_inc(s["w_copied"], 1)
                act.activation(w_t[:, L, 3, :], bank[L][:, 3 * P:], ACT.Copy, scale=tg[:, L:L + 1])\
                    .then_inc(s["w_copied"], 1)

            def attention(L):
                def step(t, par, has):
                    n = L * T + t
                    o = 1 - par
                    if has(-2):
                        wait(act, "o_tr", n - 1)
                        wait(act, "wo_mm", n - 2)
                        act.activation(o_t[:], bank[7][:, 0:P], ACT.Identity, bias=b_col[:, L, 2:3])\
                            .then_inc(s["o_copied"], 1)
                    if has(1):
                        wait(act, "xc_tr", n + 2)
                        wait(act, "qkv_mm", n)
                        act.activation(xct[:, o, :, :, :, :].rearrange("p a b c k -> p (a b) c k"),
                                       bank[4][:, 0:2 * P].rearrange("p (a k) -> p a k", k=S).unsqueeze(2)
                                       .to_broadcast([P, 2 * BT, 2, S]), ACT.Copy).then_inc(s["xc_copied"], 1)
                    if has(-1):
                        for half in range(2):
                            wait(act, "p_tr", 2 * (n - 1) + half + 1)
                            wait(act, "pv_mm", n - 1)
                            act.activation(prob_t[:, 4 * half:4 * half + 4, :], bank[2 + half][:], ACT.Copy)\
                                .then_inc(s["p_copied"], 1)
                    if has(0):
                        for half in range(2):
                            wait(act, "sub_done", 2 * n + half + 1)
                            v = prob[:, par, half * 512:(half + 1) * 512]
                            act.activation(v, v, ACT.Exp, scale=SCALE).then_inc(s["exp_done"], 1)
                    if has(2):
                        ln_apply(act, 2 * L, t + 2, par, "xc_tr", n + 1)
                return step

            run_tiles(act, attention(0), 3, 2)

            def experts(t, par, has):
                o = 1 - par
                if has(1):
                    wait(act, "mx_tr", t + 2)
                    wait(act, "hid_mm", 2 * t)
                    wait(act, "gate_mm", t)
                    act.activation(mxt[:, o, :], bank[4][:, 0:P], ACT.Copy).then_inc(s["mx_copied"], 1)
                if has(0):
                    wait(act, "gate_v", 12 * t + 3)
                    act.activation(ge[:], gl[:, 0:E], ACT.Exp, bias=gm[:]).then_inc(s["exp_gate"], 1)
                    wait(act, "hid_mm", 2 * t + 2)
                    wait(act, "y_mm", t - 1)
                    for c in range(4, EC):
                        act.activation(hid[:, par, c, :], bank[1][:, (c - 4) * P:(c - 3) * P], ACT.Relu,
                                       bias=eb1[:, c:c + 1]).then_inc(s["hid_a"], 1)
                if has(2):
                    ln_apply(act, 1, t + 2, par, "mx_tr", t + 1)

            act.wait_ge(s["moe_w_in"], 16 * MOE_LOADS)
            run_tiles(act, experts, 3, 0)
            run_tiles(act, attention(1), 3, 2)

            for k in range(TAPS):
                act.wait_ge(s["tap_tr"], k + 1)
                act.activation(f_wk[:, k, :], bank[k][:], ACT.Copy).then_inc(s["tap_copied"], 1)
            act.wait_ge(s["tap_tr"], TAPS + 1)
            act.activation(f_w2t[:].rearrange("p c d -> p (c d)"), bank[3][:], ACT.Copy).then_inc(s["w2t_copied"], 1)

            def ffn(t, par, has):
                o = 1 - par
                if has(2):
                    ln_apply(act, 3, t + 2, par, "q1_done", t + 1)
                if has(1):
                    wait(act, "xq_tr", t + 2)
                    wait(act, "conv_mm", t)
                    src = bank[4][:, 0:P].rearrange("p (b s) -> p b s", b=BT)
                    act.activation(xtap[:, o, 0, :, 1:S], src[:, :, 0:S - 1], ACT.Copy)
                    act.activation(xtap[:, o, 1, :, :], src, ACT.Copy)
                    act.activation(xtap[:, o, 2, :, 0:S - 1], src[:, :, 1:S], ACT.Copy).then_inc(s["xq_copied"], 1)
                if has(0):
                    wait(act, "hpre_done", t + 1)
                    wait(act, "q2_ready", t - 1)
                    act.activation(hact[:, par, :], hpre[:, par, :], ACT.Silu).then_inc(s["silu_done"], 1)
                if has(0):
                    wait(act, "a2_ready", t + 1)
                    wait(act, "q2_tr", t - 1)
                    act.activation(q2[:, par, :], hact[:, par, :], ACT.Identity, scale=a2s[:, par, :],
                                   bias=const[:, C_RND:C_RND + 1]).then_inc(s["q2_ready"], 1)
                if has(2):
                    wait(act, "q1_ready", t + 3)
                    wait(act, "xq_ready", t + 2)
                    act.activation(q1[:], xn[:, par, :], ACT.Identity, scale=a1[:, par, 3:4],
                                   bias=const[:, C_RND:C_RND + 1]).then_inc(s["q1_done"], 1)

            run_tiles(act, ffn, 3, 0)

        @block.vector
        def _(dve):
            dve.wait_ge(s["const_in"], 16)
            dve.tensor_copy(ident16[:], ident).then_inc(s["ident16_done"], 1)
            for par in range(2):
                for b in range(BT):
                    dve.tensor_copy(vb[:, par, :, b, :, HD:VW],
                                    const[:, C_H:C_H + 2].unsqueeze(1).unsqueeze(3).to_broadcast([P, NPAIR, 2, 1]))\
                        .then_inc(s["ones_set"], 1)
            dve.wait_ge(s["attn_w_in"], 16 * 16)
            dve.wait_ge(s["tanh_done"], 1)
            for L in range(2):
                dve.tensor_scalar(bo_row[:, L, :], bo_row[:, L, :], tg[:, L:L + 1], None, ALU.mult)\
                    .then_inc(s["setup_v"], 1)
            dve.tensor_copy(q_mask[:, 0, :, :], const[:, C_R:C_R + RQ].unsqueeze(2).to_broadcast([P, RQ, P]))\
                .then_inc(s["setup_v"], 1)
            dve.wait_ge(s["mask_in"], 32)
            dve.tensor_scalar(m_keep[:], m_int[:], 0.0, None, ALU.not_equal).then_inc(s["mask_v"], 1)
            dve.wait_ge(s["mask_v"], 1)
            dve.tensor_reduce(m_any[:], m_keep[:], AX.X, ALU.max).then_inc(s["mask_v"], 1)
            dve.wait_ge(s["mask_v"], 2)
            dve.tensor_scalar(m_dead[:], m_any[:], -1.0, 1.0, ALU.mult, ALU.add).then_inc(s["mask_v"], 1)
            dve.tensor_scalar(m_diag[:], const[0:S, C_ID:C_ID + S], m_any[0:S, :], None, ALU.mult)\
                .then_inc(s["mask_v"], 1)
            dve.wait_ge(s["mask_v"], 4)
            dve.tensor_scalar(m_keep2[:], m_keep[:], m_dead[:], 1.0, ALU.max, ALU.subtract).then_inc(s["mask_v"], 1)
            dve.wait_ge(s["mask_v"], 5)
            dve.tensor_scalar(neg_mask[:], m_keep2[:], NEG, None, ALU.mult).then_inc(s["mask_v"], 1)
            dve.wait_ge(s["alive_mm"], 1)
            for r in range(RQ):
                dve.tensor_scalar(q_mask[:, 1, r, :].rearrange("p (b s) -> p b s", b=BT),
                                  bank[6][:, 0:S].unsqueeze(1).to_broadcast([P, BT, S]),
                                  const[:, C_R + r:C_R + r + 1], None, ALU.mult).then_inc(s["setup_v"], 1)

            def attention(L):
                def step(t, par, has):
                    n = L * T + t
                    o = 1 - par
                    if has(0):
                        for half in range(2):
                            wait(dve, "scores_mm", 2 * n + half + 1)
                            sc = bank[half][:].rearrange("p (h k) -> p h k", k=S)
                            m = smax[:, half * 8:half * 8 + 8]
                            wait(dve, "sub_done", 2 * n + half - 1)
                            dve.tensor_reduce(m, sc, AX.X, ALU.max).then_inc(s["smax_done"], 1)
                            dve.wait_ge(s["smax_done"], 2 * n + half + 1)
                            wait(dve, "p_tr", 2 * (n - 1))
                            dve.tensor_tensor(prob[:, par, half * 512:(half + 1) * 512].rearrange("p (h k) -> p h k", k=S),
                                              sc, m.unsqueeze(2).to_broadcast([P, 8, S]), ALU.subtract)\
                                .then_inc(s["sub_done"], 1)
                    if has(-2):
                        wait(dve, "wo_mm", n - 1)
                        wait(dve, "bo_added", n - 1)
                        dve.tensor_tensor(x_tile(t - 2), bank[7][:, P:2 * P], x_tile(t - 2), ALU.add)\
                            .then_inc(s["x_attn"], 1)
                    if has(1):
                        wait(dve, "qkv_mm", n + 2)
                        wait(dve, "scores_mm", 2 * n)
                        dve.scalar_tensor_tensor(
                            out=qq[:, o, :, :], in0=bank[5][:, 0:P].unsqueeze(1).to_broadcast([P, RQ, P]),
                            scalar=b_col[:, L, 0:1], in1=q_mask[:, L, :, :], op0=ALU.add, op1=ALU.mult)\
                            .then_inc(s["qk_ready"], 1)
                        dve.scalar_tensor_tensor(
                            out=kj[:, o, :, :], in0=bank[5][:, P:2 * P].unsqueeze(1).to_broadcast([P, JH, P]),
                            scalar=b_col[:, L, 1:2],
                            in1=const[:, C_J:C_J + JH].unsqueeze(2).to_broadcast([P, JH, P]),
                            op0=ALU.add, op1=ALU.mult).then_inc(s["qk_ready"], 1)
                    if has(-1):
                        wait(dve, "pv_mm", n)
                        wait(dve, "o_tr", n - 2)
                        ov = bank[6][:, 0:NPAIR * BT * 2 * VW].rearrange("p (i b h v) -> p i b h v", i=NPAIR, b=BT, h=2)
                        rv = rden[:].rearrange("p (i h) -> p i h", h=2)
                        onv = o_n[:, o, :].rearrange("p (i h v) -> p i h v", i=NPAIR, h=2)
                        wait(dve, "o_norm", 2 * (n - 1))
                        for b in range(BT):
                            q = slice(b * S, (b + 1) * S)
                            dve.reciprocal(rv[q], ov[q, :, b, :, HD]).then_inc(s["rden_done"], 1)
                        dve.wait_ge(s["rden_done"], 2 * n)
                        for b in range(BT):
                            q = slice(b * S, (b + 1) * S)
                            dve.tensor_tensor(onv[q], ov[q, :, b, :, 0:HD],
                                              rv[q].unsqueeze(3).to_broadcast([S, NPAIR, 2, HD]), ALU.mult)\
                                .then_inc(s["o_norm"], 1)
                    if has(1):
                        wait(dve, "pv_mm", n)
                        for b in range(BT):
                            dve.tensor_tensor(
                                vb[:, o, :, b, :, 0:HD],
                                bank[5][:, (2 + b) * P:(3 + b) * P].rearrange("p (i h v) -> p i h v", i=NPAIR, h=2),
                                const[:, C_H:C_H + 2].unsqueeze(1).unsqueeze(3).to_broadcast([P, NPAIR, 2, HD]),
                                ALU.mult).then_inc(s["v_ready"], 1)
                    if has(3):
                        ln_stats(dve, 2 * L, t + 3, o)
                return step

            run_tiles(dve, attention(0), 3, 2)

            dve.wait_ge(s["moe_w_in"], 16 * MOE_LOADS)
            dve.tensor_scalar(thr[:], const[:, C_THR:C_THR + E - 1], dp_b2[:], None, ALU.subtract)\
                .then_inc(s["setup_v"], 1)
            dve.wait_ge(s["setup_v"], 8)

            def experts(t, par, has):
                o = 1 - par
                if has(0):
                    G = 12 * t

                    def gate(ins):
                        ins.then_inc(s["gate_v"], 1)

                    wait(dve, "gate_mm", t + 1)
                    wait(dve, "exp_gate", t)
                    lg = gl[:, 0:E]
                    gate(dve.tensor_tensor(gl[:], bank[5][:, 0:GW], gate_b[:], ALU.add))
                    dve.wait_ge(s["gate_v"], G + 1)
                    gate(dve.scalar_tensor_tensor(out=gj[:], in0=gl[:, E:GW], scalar=0.0, in1=dp_w2[:],
                                                  op0=ALU.max, op1=ALU.mult, accum_out=gz[:]))
                    gate(dve.tensor_reduce(gm[:], lg, AX.X, ALU.max, negate=True))
                    l_row = lg.unsqueeze(1).to_broadcast([P, E, E])
                    l_col = lg.unsqueeze(2).to_broadcast([P, E, E])
                    tie = const[:, C_TIE:C_TIE + E * E].rearrange("p (e f) -> p e f", e=E)
                    gate(dve.tensor_tensor(g_gt[:], l_row, l_col, ALU.is_gt))
                    gate(dve.tensor_tensor(g_eq[:], l_row, l_col, ALU.is_equal))
                    dve.wait_ge(s["gate_v"], G + 5)
                    gate(dve.tensor_tensor(g_eq[:], g_eq[:], tie, ALU.mult))
                    gate(dve.tensor_scalar(gs3[:], thr[:], gz[:], 1.0, ALU.is_le, ALU.add, accum_out=gk[:]))
                    dve.wait_ge(s["gate_v"], G + 7)
                    gate(dve.tensor_tensor(g_gt[:], g_gt[:], g_eq[:], ALU.add))
                    dve.wait_ge(s["gate_v"], G + 8)
                    gate(dve.tensor_reduce(g_rank[:], g_gt[:], AX.X, ALU.add))
                    wait(dve, "hid_mm", 2 * t + 1)
                    wait(dve, "y_mm", t - 1)
                    for c in range(4):
                        dve.tensor_scalar(hid[:, par, c, :], bank[0][:, c * P:(c + 1) * P], eb1[:, c:c + 1], 0.0,
                                          ALU.add, ALU.max).then_inc(s["hid_v"], 1)
                    wait(dve, "exp_gate", t + 1)
                    dve.wait_ge(s["gate_v"], G + 9)
                    gate(dve.scalar_tensor_tensor(out=g_ew[:], in0=g_rank[:], scalar=gk[:], in1=ge[:],
                                                  op0=ALU.is_lt, op1=ALU.mult, accum_out=g_sum[:]))
                    dve.wait_ge(s["gate_v"], G + 10)
                    gate(dve.reciprocal(g_rs[:], g_sum[:]))
                    dve.wait_ge(s["gate_v"], G + 11)
                    wait(dve, "y_v", 4 * (t - 1))
                    wait(dve, "eb_added", t - 1)
                    gate(dve.tensor_scalar(g_ew[:], g_ew[:], g_rs[:], None, ALU.mult))
                    dve.wait_ge(s["gate_v"], G + 12)
                    dve.tensor_scalar(gwt[:, par, :], g_ew[:], tg[:, 2:3], None, ALU.mult).then_inc(s["gate_done"], 1)
                if has(-1):
                    wait(dve, "y_mm", t)
                    wait(dve, "eb_added", t)
                    for e in range(E):
                        src = x_tile(t - 1) if e == 0 else y_acc[:, (e - 1) % 2, :]
                        dst = x_tile(t - 1) if e == E - 1 else y_acc[:, e % 2, :]
                        if e:
                            dve.wait_ge(s["y_v"], 4 * (t - 1) + e)
                        else:
                            wait(dve, "gate_done", t)
                        ins = dve.scalar_tensor_tensor(out=dst, in0=bank[6][:, e * P:(e + 1) * P],
                                                       scalar=gwt[:, o, e:e + 1], in1=src, op0=ALU.mult, op1=ALU.add)
                        ins.then_inc(s["y_v"], 1)
                if has(3):
                    ln_stats(dve, 1, t + 3, o)

            run_tiles(dve, experts, 3, 1)
            run_tiles(dve, attention(1), 3, 2)

            dve.wait_ge(s["ffn_w_in"], 64)
            dve.tensor_reduce(f_s[:, 0:1], f_w1[:].rearrange("p c d -> p (c d)"), AX.X, ALU.add,
                              apply_absolute_value=True).then_inc(s["ffn_sum"], 1)
            dve.tensor_reduce(f_s[:, 1:2], f_w2[:], AX.X, ALU.add, apply_absolute_value=True)\
                .then_inc(s["ffn_sum"], 1)
            dve.wait_ge(s["sum_mm"], 1)
            k = [0]

            def tern(ins):
                k[0] += 1
                ins.then_inc(s["tern"], 1)
                dve.wait_ge(s["tern"], k[0])

            tern(dve.tensor_scalar(f_s[:, 2:4], bank[6][:, 0:2], 1.0 / (F * D), Q_EPS, ALU.mult, ALU.max))
            tern(dve.reciprocal(f_s[:, 4:6], f_s[:, 2:4]))
            for w, i in ((f_w1[:].rearrange("p c d -> p (c d)"), 0), (f_w2[:], 1)):
                tern(dve.tensor_scalar(w, w, f_s[:, 4 + i:5 + i], ROUND, ALU.mult, ALU.add))
                tern(dve.tensor_scalar(w, w, ROUND, 1.0, ALU.subtract, ALU.min))
                tern(dve.tensor_scalar(w, w, -1.0, None, ALU.max))
            tern(dve.tensor_scalar(f_cw[:], f_cw[:], f_s[:, 2:3], None, ALU.mult))
            tern(dve.tensor_scalar(f_s[:, 6:7], f_s[:, 3:4], tg[:, 3:4], 1.0 / 127.0, ALU.mult, ALU.mult))
            for tap in range(TAPS):
                for c in range(FC):
                    dve.tensor_scalar(f_tap[:, tap, c, :], f_w1[:, c, :], f_cw[:, c, tap:tap + 1], None, ALU.mult)\
                        .then_inc(s["tap_ready"], 1)

            def ffn(t, par, has):
                o = 1 - par
                if has(2):
                    m = 4 * (t + 2)
                    wait(dve, "xn_ready", 3 * T + t + 3)
                    wait(dve, "q1_done", t + 1)
                    dve.tensor_reduce(a1[:, par, 0:1], xn[:, par, :], AX.X, ALU.max, apply_absolute_value=True)\
                        .then_inc(s["q1_v"], 1)
                    dve.wait_ge(s["q1_v"], m + 1)
                    dve.tensor_scalar(a1[:, par, 1:2], a1[:, par, 0:1], Q_EPS, None, ALU.max).then_inc(s["q1_v"], 1)
                    dve.wait_ge(s["q1_v"], m + 2)
                    dve.reciprocal(a1[:, par, 2:3], a1[:, par, 1:2]).then_inc(s["q1_v"], 1)
                    dve.tensor_scalar(a1i[:, par, :], a1[:, par, 1:2], 1.0 / 127.0, None, ALU.mult).then_inc(s["q1_v"], 1)
                    dve.wait_ge(s["q1_v"], m + 4)
                    dve.tensor_scalar(a1[:, par, 3:4], a1[:, par, 2:3], 127.0, None, ALU.mult).then_inc(s["q1_ready"], 1)
                if has(-1):
                    wait(dve, "q2_tr", t)
                    wait(dve, "out_mm", t - 2)
                    dve.tensor_scalar(q2t[:, o, :], bank[5][:], ROUND, 127.0, ALU.subtract, ALU.min)\
                        .then_inc(s["q2_copied"], 1)
                if has(0):
                    wait(dve, "conv_mm", t + 1)
                    wait(dve, "silu_done", t - 1)
                    dve.tensor_tensor(hpre[:, par, :], bank[par][:], f_cb[:], ALU.add).then_inc(s["hpre_done"], 1)
                if has(-2):
                    wait(dve, "out_mm", t - 1)
                    dve.scalar_tensor_tensor(out=x_tile(t - 2), in0=bank[6][:, 0:P], scalar=a2f[:, par, :],
                                             in1=x_tile(t - 2), op0=ALU.mult, op1=ALU.add).then_inc(s["x_out"], 1)
                if has(0):
                    m = 3 * t
                    wait(dve, "silu_done", t + 1)
                    wait(dve, "q2_ready", t - 1)
                    wait(dve, "a2_ready", t)
                    dve.tensor_reduce(a2[:, 0:1], hact[:, par, :], AX.X, ALU.max, apply_absolute_value=True)\
                        .then_inc(s["a2_v"], 1)
                    dve.wait_ge(s["a2_v"], m + 1)
                    dve.tensor_scalar(a2[:, 1:2], a2[:, 0:1], Q_EPS, None, ALU.max).then_inc(s["a2_v"], 1)
                    dve.wait_ge(s["a2_v"], m + 2)
                    dve.reciprocal(a2[:, 2:3], a2[:, 1:2]).then_inc(s["a2_v"], 1)
                    wait(dve, "x_out", t - 1)
                    dve.tensor_scalar(a2f[:, par, :], a2[:, 1:2], f_s[:, 6:7], None, ALU.mult)
                    dve.wait_ge(s["a2_v"], m + 3)
                    dve.tensor_scalar(a2s[:, par, :], a2[:, 2:3], 127.0, None, ALU.mult).then_inc(s["a2_ready"], 1)
                if has(2):
                    wait(dve, "q1_done", t + 3)
                    wait(dve, "xq_tr", t + 1)
                    dve.tensor_scalar(xdq[:, par, :], q1[:], ROUND, a1i[:, par, :], ALU.subtract, ALU.mult)\
                        .then_inc(s["xq_ready"], 1)
                if has(3):
                    ln_stats(dve, 3, t + 3, o)

            run_tiles(dve, ffn, 3, 2)

        @block.tensor
        def _(pe):
            def tr(dst, src):
                return pe.transpose(dst, src, ident)

            pe.wait_ge(s["const_in"], 16)
            pe.wait_ge(s["attn_w_in"], 16 * 16)
            for L in range(2):
                for n in range(4):
                    last = tr(bank[L][:, n * P:(n + 1) * P], w_raw[:, L, n, :])
                last.then_inc(s["w_tr"], 1)
            pe.wait_ge(s["mask_v"], 4)
            pe.matmul(bank[6][:, 0:S], ones[0:S, :], m_diag[:], start=True, stop=True).then_inc(s["alive_mm"], 1)
            pe.wait_ge(s["w_copied"], 4)
            pe.wait_ge(s["setup_v"], 7)
            pe.wait_ge(s["mask_v"], 6)
            pe.wait_ge(s["ident16_done"], 1)
            pe.wait_ge(s["ones_set"], 5)

            def attention(L):
                def step(t, par, has):
                    n = L * T + t
                    o = 1 - par
                    if has(0):
                        wait(pe, "qk_ready", 2 * n + 2)
                        for half in range(2):
                            wait(pe, "sub_done", 2 * n + half - 1)
                            if L == 1:
                                pe.matmul(bank[half][:].rearrange("p (h k) -> p h k", k=S), ident16[:],
                                          neg_mask[:].unsqueeze(1).to_broadcast([P, 8, S]),
                                          start=True, stop=False, skip_group_check=True)
                            for rr in range(2):
                                r = half * 2 + rr
                                for b in range(BT):
                                    q = slice(b * S, (b + 1) * S)
                                    last = pe.matmul(bank[half][q, rr * 256:(rr + 1) * 256], qq[:, par, r, q],
                                                     kj[:, par, :, q], start=(L == 0), stop=True,
                                                     skip_group_check=True)
                            last.then_inc(s["scores_mm"], 1)
                    if has(-2):
                        wait(pe, "o_norm", 2 * (n - 1))
                        wait(pe, "x_attn", n - 2)
                        tr(bank[7][:, 0:P], o_n[:, par, :]).then_inc(s["o_tr"], 1)
                    if has(1):
                        wait(pe, "xn_ready", 2 * L * T + t + 2)
                        wait(pe, "xc_copied", n + 1)
                        tr(bank[4][:, 0:P], xn[:, o, :])
                        pe.wait_ge(ctx_ld[o], L * T * 8 + (t + 1 + 1 + par) * 8)
                        tr(bank[4][:, P:2 * P], ctx_in[:, o, :]).then_inc(s["xc_tr"], 1)
                    if has(-1):
                        for half in range(2):
                            wait(pe, "exp_done", 2 * (n - 1) + half + 1)
                            wait(pe, "p_copied", 2 * (n - 2) + half + 1)
                            for i in range(4):
                                c = (half * 4 + i) * P
                                last = tr(bank[2 + half][:, i * P:(i + 1) * P], prob[:, o, c:c + P])
                            last.then_inc(s["p_tr"], 1)
                    if has(1):
                        wait(pe, "xc_copied", n + 2)
                        wait(pe, "qk_ready", 2 * n + 2)
                        wait(pe, "v_ready", 2 * n + 2)
                        pe.matmul(bank[5][:, 0:P], w_t[:, L, 0, :], xct[:, o, 0, :, 0, :], start=True, stop=True)
                        pe.matmul(bank[5][:, P:2 * P], w_t[:, L, 1, :], xct[:, o, 1, :, 0, :], start=True, stop=True)
                        for b in range(BT):
                            keys = xct[:, o, 1, b, :, :].rearrange("p c k -> p (c k)")
                            last = pe.matmul(bank[5][:, (2 + b) * P:(3 + b) * P], keys, w_t[:, L, 2, :],
                                             start=True, stop=True)
                        last.then_inc(s["qkv_mm"], 1)
                    if has(-2):
                        wait(pe, "o_copied", n - 1)
                        pe.matmul(bank[7][:, P:2 * P], o_t[:], w_t[:, L, 3, :], start=True, stop=True)\
                            .then_inc(s["wo_mm"], 1)
                    if has(-1):
                        wait(pe, "p_copied", 2 * n)
                        wait(pe, "v_ready", 2 * n)
                        wait(pe, "o_norm", 2 * (n - 1))
                        for i in range(NPAIR):
                            w = BT * 2 * VW
                            last = pe.matmul(bank[6][:, i * w:(i + 1) * w], prob_t[:, i, :],
                                             vb[:, o, i, :, :, :].rearrange("p b h v -> p (b h v)"),
                                             start=True, stop=True)
                        last.then_inc(s["pv_mm"], 1)
                return step

            run_tiles(pe, attention(0), 3, 2)

            def experts(t, par, has):
                o = 1 - par
                if has(1):
                    wait(pe, "xn_ready", T + t + 2)
                    wait(pe, "mx_copied", t + 1)
                    tr(bank[4][:, 0:P], xn[:, o, :]).then_inc(s["mx_tr"], 1)
                if has(0):
                    wait(pe, "mx_copied", t + 1)
                    wait(pe, "gate_v", 12 * t - 11)
                    pe.matmul(bank[5][:, 0:GW], mxt[:, par, :], gate_w[:], start=True, stop=True)\
                        .then_inc(s["gate_mm"], 1)
                    for half in range(2):
                        wait(pe, "hid_v" if half == 0 else "hid_a", 4 * t)
                        for c in range(4):
                            last = pe.matmul(bank[half][:, c * P:(c + 1) * P], ew1[:, half * 4 + c, :],
                                             mxt[:, par, :], start=True, stop=True)
                        last.then_inc(s["hid_mm"], 1)
                if has(-1):
                    wait(pe, "hid_v", 4 * t)
                    wait(pe, "hid_a", 4 * t)
                    wait(pe, "y_v", 4 * (t - 1))
                    for e in range(E):
                        for c in range(2):
                            last = pe.matmul(bank[6][:, e * P:(e + 1) * P], hid[:, o, 2 * e + c, :],
                                             ew2[:, 2 * e + c, :], start=(c == 0), stop=(c == 1))
                    last.then_inc(s["y_mm"], 1)

            pe.wait_ge(s["x_attn"], T)
            pe.wait_ge(s["moe_w_in"], 16 * MOE_LOADS)
            run_tiles(pe, experts, 3, 1)
            pe.wait_ge(s["y_v"], 4 * T)
            run_tiles(pe, attention(1), 3, 2)
            pe.wait_ge(s["x_attn"], 2 * T)

            pe.wait_ge(s["ffn_sum"], 2)
            pe.matmul(bank[6][:, 0:2], ones, f_s[:, 0:2], start=True, stop=True).then_inc(s["sum_mm"], 1)
            for tap in range(TAPS):
                pe.wait_ge(s["tap_ready"], FC * (tap + 1))
                for c in range(FC):
                    last = tr(bank[tap][:, c * P:(c + 1) * P], f_tap[:, tap, c, :])
                last.then_inc(s["tap_tr"], 1)
            for c in range(FC):
                last = tr(bank[3][:, c * P:(c + 1) * P], f_w2[:, c * P:(c + 1) * P])
            last.then_inc(s["tap_tr"], 1)
            pe.wait_ge(s["tap_copied"], TAPS)
            pe.wait_ge(s["w2t_copied"], 1)

            def ffn(t, par, has):
                o = 1 - par
                if has(1):
                    wait(pe, "xq_ready", t + 2)
                    wait(pe, "xq_copied", t + 1)
                    tr(bank[4][:, 0:P], xdq[:, o, :]).then_inc(s["xq_tr"], 1)
                if has(0):
                    wait(pe, "xq_copied", t + 1)
                    wait(pe, "hpre_done", t - 1)
                    for tap in range(TAPS):
                        last = pe.matmul(bank[par][:], xtap[:, par, tap, :, :].rearrange("p b s -> p (b s)"), f_wk[:, tap, :],
                                         start=(tap == 0), stop=(tap == TAPS - 1))
                    last.then_inc(s["conv_mm"], 1)
                if has(-2):
                    wait(pe, "q2_copied", t - 1)
                    wait(pe, "x_out", t - 2)
                    for c in range(FC):
                        last = pe.matmul(bank[6][:, 0:P], q2t[:, par, c * P:(c + 1) * P], f_w2t[:, c, :],
                                         start=(c == 0), stop=(c == FC - 1))
                    last.then_inc(s["out_mm"], 1)
                if has(-1):
                    wait(pe, "q2_ready", t)
                    wait(pe, "q2_copied", t - 1)
                    for c in range(FC):
                        last = tr(bank[5][:, c * P:(c + 1) * P], q2[:, o, c * P:(c + 1) * P])
                    last.then_inc(s["q2_tr"], 1)

            run_tiles(pe, ffn, 3, 2)


def constants(np):
    c = np.zeros((P, C_ALL), np.float32)
    p = np.arange(P)
    c[:, C_ID:C_ID + P] = np.eye(P)
    c[:, C_ONE:C_ONE + P] = 1
    for j in range(JH):
        c[:, C_J + j] = (p // HD) % JH == j
    for r in range(RQ):
        c[:, C_R + r] = p // (JH * HD) == r
    for h in range(2):
        c[:, C_H + h] = p // S == h
    for e in range(E):
        for f in range(E):
            c[:, C_TIE + e * E + f] = f < e
    for i, v in enumerate((0.75, 1.25, 1.75)):
        z = np.float32(math.log(math.expm1(v)))
        c[:, C_THR + i] = np.nextafter(z, np.float32(2)) if i == 1 else z
    c[:, C_POW] = -0.5
    c[:, C_RND] = ROUND
    return c


_INS = ['x', 'ctx_1024', 'mask_1x1xSxS2_ik0', 'g_xattn', 'g_ffn'] + [
    f"L{L}_xattn_{w}{c}" for L in range(2) for c in "qkvo" for w in "Wb"] + [
    f"L0_ffn_{n}" for n in ("gate_w", "gate_b", "dp_w1", "dp_b1", "dp_w2", "dp_b2", "ew1", "eb1", "ew2", "eb2")] + [
    f"L1_ffn_{n}" for n in ("w1", "conv_w", "conv_b", "w2")]


def kernel(**inputs):
    import numpy as np
    import concourse.bacc as bacc
    from concourse.bass_utils import run_bass_kernel_spmd

    nc = bacc.Bacc("TRN2", target_bir_lowering=False, num_devices=1)
    arrays, aps = {}, {}
    for name in _INS:
        v = np.ascontiguousarray(inputs[name])
        arrays[f"in_{name}"] = v
        aps[name] = nc.dram_tensor(f"in_{name}", v.shape, mybir.dt.from_np(v.dtype), kind="ExternalInput").ap()
    arrays["in_const"] = constants(np)
    aps["const"] = nc.dram_tensor("in_const", (P, C_ALL), F32, kind="ExternalInput").ap()
    out = nc.dram_tensor("out_x", (B, S, D), F32, kind="ExternalOutput").ap()
    build(nc, aps, out)
    r = run_bass_kernel_spmd(nc, [arrays], core_ids=[0])
    return r.results[0]["out_x"]
```

```python
import math

import concourse.bass as bass
from concourse import mybir
from contextlib import ExitStack

F32 = mybir.dt.float32
BF16 = mybir.dt.bfloat16
F32R = mybir.dt.float32r
I32 = mybir.dt.int32
ALU = mybir.AluOpType
ACT = mybir.ActivationFunctionType
AX = mybir.AxisListType

P = 128
B, S, D = 128, 64, 128
H, HD = 16, 8
BT = P // S
T = B // BT
NPAIR = H // 2
JH, RQ = 4, 4
E, HE = 4, 256
EC = E * HE // P
DPH = 64
G = 4
NG = T // G
GW = E + DPH
F = 512
FC = F // P
TAPS = 3
VW = HD + 1
LN_EPS = 1e-5
Q_EPS = 1e-5
SCALE = 1.0 / math.sqrt(HD)
NEG = 1e30
ROUND = 1.5 * 2.0 ** 23

C_ID, C_ONE, C_J, C_R, C_H, C_TIE, C_THR, C_POW, C_RND, C_EPS, C_NEG = \
    0, 128, 256, 260, 264, 266, 282, 285, 286, 287, 288
C_ALL = 289


def build(nc, a, out):
    with ExitStack() as ctx:
        def sb(name, shape, dt=F32):
            return ctx.enter_context(nc.sbuf_tensor(name, shape, dt))

        def sem(name):
            return ctx.enter_context(nc.semaphore(name))

        bank = [ctx.enter_context(nc.psum_tensor(f"bank{i}", [P, 512], F32)) for i in range(8)]

        const = sb("const", [P, C_ALL])
        ident = const[:, C_ID:C_ID + P]
        ones = const[:, C_ONE:C_ONE + P]
        ident16 = sb("ident16", [P, P], BF16)
        x_all = sb("x_all", [P, T * D])
        tg = sb("tg", [P, 4])
        graw = sb("graw", [P, 4])

        w_raw = sb("w_raw", [P, 2, 4, P])
        w_t = sb("w_t", [P, 2, 4, P])
        b_col = sb("b_col", [P, 2, 3])
        bo_row = sb("bo_row", [P, 2, P])
        q_mask = sb("q_mask", [P, 2, RQ, P])
        neg_mask = sb("neg_mask", [P, S], BF16)
        m_int = sb("m_int", [P, S], I32)
        m_keep = sb("m_keep", [P, S])
        m_any = sb("m_any", [P, 1])
        m_dead = sb("m_dead", [P, 1])
        m_keep2 = sb("m_keep2", [P, S])
        m_diag = sb("m_diag", [S, S])

        gate_w = sb("gate_w", [P, GW])
        gate_b = sb("gate_b", [P, GW])
        dp_w2 = sb("dp_w2", [P, DPH])
        dp_b2 = sb("dp_b2", [P, 1])
        thr = sb("thr", [P, E - 1])
        ew1 = sb("ew1", [P, E, HE])
        eb1 = sb("eb1", [P, EC])
        ew2 = sb("ew2", [P, EC, P])
        eb2 = sb("eb2", [P, E * P])

        f_w1 = sb("f_w1", [P, FC, D])
        f_w2 = sb("f_w2", [P, F])
        f_cw = sb("f_cw", [P, FC, TAPS])
        f_cb = sb("f_cb", [P, F])
        f_tap = sb("f_tap", [P, TAPS, FC, D])
        f_wk = sb("f_wk", [P, TAPS, F])
        f_w2t = sb("f_w2t", [P, FC, D], BF16)
        f_s = sb("f_s", [P, 8])

        ln_st = sb("ln_st", [P, 2, 6])
        ln_mv = sb("ln_mv", [P, 2, 2])
        ln_ve = sb("ln_ve", [P, 2, 1])
        ln_nm = sb("ln_nm", [P, 2, 1])
        ln_rs = sb("ln_rs", [P, 2, 1])
        ln_nr = sb("ln_nr", [P, 2, 1])
        xn = sb("xn", [P, 2, D])

        ctx_in = sb("ctx_in", [P, 2, D])
        xct = sb("xct", [P, 2, 2, BT, 2, S])
        qq = sb("qq", [P, 2, RQ, P])
        kj = sb("kj", [P, 2, JH, P])
        vb = sb("vb", [P, 2, NPAIR, BT, 2, VW])
        smax = sb("smax", [P, H])
        prob = sb("prob", [P, 2, H * S])
        prob_t = sb("prob_t", [P, NPAIR, P])
        rden = sb("rden", [P, H])
        o_n = sb("o_n", [P, 2, P])
        o_t = sb("o_t", [P, P])

        m_st = sb("m_st", [P, 2, G, 6])
        m_mv = sb("m_mv", [P, 2, G, 2])
        m_ve = sb("m_ve", [P, 2, G])
        m_nm = sb("m_nm", [P, 2, G])
        m_rs = sb("m_rs", [P, 2, G])
        m_nr = sb("m_nr", [P, 2, G])
        m_xn = sb("m_xn", [P, G, D])
        mxt = sb("mxt", [P, G * P])
        mx_hi = sb("mx_hi", [P, 2, G * P], F32R)
        mx_lo = sb("mx_lo", [P, 2, G * P], F32R)
        ew1_hi = sb("ew1_hi", [P, EC, P], F32R)
        ew1_lo = sb("ew1_lo", [P, EC, P], F32R)
        hid = sb("hid", [P, EC, G * P])
        gl = sb("gl", [P, G, GW])
        gj = sb("gj", [P, G, DPH])
        gz = sb("gz", [P, G])
        gk = sb("gk", [P, G])
        gs3 = sb("gs3", [P, G, E - 1])
        gm = sb("gm", [P, G])
        gls = sb("gls", [P, G, E])
        ge = sb("ge", [P, G, E])
        g_gt = sb("g_gt", [P, G, E, E])
        g_eq = sb("g_eq", [P, G, E, E])
        g_rank = sb("g_rank", [P, G, E])
        g_sel = sb("g_sel", [P, G, E])
        g_ew = sb("g_ew", [P, G, E])
        g_sum = sb("g_sum", [P, G])
        g_rs = sb("g_rs", [P, G])
        gwt = sb("gwt", [P, 2, G, E])
        eb_t = sb("eb_t", [P, 2, E, P])
        eb_acc = sb("eb_acc", [P, 2, P])
        eb_sum = sb("eb_sum", [P, P])
        y_acc = sb("y_acc", [P, 2, P])

        sc_m = sb("sc_m", [P, 2])
        sc_c = sb("sc_c", [P, 2])
        sc_r = sb("sc_r", [P, 2])
        sc_q = sb("sc_q", [P, 2, 2])
        sc_i = sb("sc_i", [P, 2, 2])
        sc_l = sb("sc_l", [P, 1])
        sc_f = sb("sc_f", [P, 2])
        q1 = sb("q1", [P, D])
        xdq = sb("xdq", [P, 2, D])
        xtap = sb("xtap", [P, 2, TAPS, BT, S])
        hpre = sb("hpre", [P, 2, F])
        hact = sb("hact", [P, 2, F])
        q2 = sb("q2", [P, 2, F])
        q2t = sb("q2t", [P, 2, F], BF16)

        names = """const_in attn_w_in moe_w_in ffn_w_in g_in mask_in
            tanh_done ident16_done w_tr w_copied setup_v mask_v alive_mm ones_set
            sum_mm ffn_sum tern tap_ready tap_tr tap_copied w2t_copied setup_act
            ln ln_mv ln_ready xn_ready
            xc_tr xc_copied qkv_mm qk_ready v_ready scores_mm smax_done sub_done exp_done
            p_tr p_copied pv_mm rden_done o_norm o_tr o_copied wo_mm bo_added x_attn
            m_ln m_mean m_ready m_xn_ready ew1_split
            mx_tr mx_copied mx_hi_done mx_lo_done hid_mm gate_mm relu_v relu_a gate_v exp_gate gate_done
            eb_mult eb_v eb_added y_mm y_v
            x_max h_max sc_v sc_ready sc_late sc_set q1_done xq_ready xq_tr xq_copied conv_mm hpre_done silu_done q2_ready
            q2_tr q2_copied out_mm x_out""".split()
        s = {n: sem(n) for n in names}
        x_in = [sem(f"x_in{i}") for i in range(2)]
        ctx_ld = [sem(f"ctx_ld{i}") for i in range(2)]
        stored = sem("stored")

        def wait(eng, name, value):
            if isinstance(value, int) and value <= 0:
                return
            eng.wait_ge(s[name], value)

        def run_tiles(eng, step, lead, lag, lo=2, T=T):
            n = (T - lead - lo) // 2
            for t in range(-lead, lo):
                step(t, t % 2, lambda k: 0 <= t + k < T)
            with eng.Fori(0, n) as i:
                for par in range(2):
                    step(i * 2 + (lo + par), par, lambda k: True)
            for t in range(lo + 2 * n, T + lag):
                step(t, t % 2, lambda k: 0 <= t + k < T)

        LN0 = {0: 0, 2: T, 3: 2 * T}

        def x_tile(t):
            return x_all[:, bass.ds(t * D, D)]

        def ln_stats(dve, f, t, par):
            n = LN0[f] + t
            if f == 0:
                dve.wait_ge(x_in[par], (t + (2 - par)) * 8)
            else:
                wait(dve, {2: "y_v", 3: "x_attn"}[f], {2: E * (t + 1), 3: T + t + 1}[f])
            wait(dve, "ln_mv", n - 1)
            dve.bn_stats(ln_st[:, par, :], x_tile(t)).then_inc(s["ln"], 1)

        def ln_mean_ready(dve, f, t):
            n = LN0[f] + t
            wait(dve, "ln_ready", LN_STEPS * (n - 1))
            wait(dve, "ln", n + 1)

        def ln_mean(dve, par):
            dve.bn_aggr(ln_mv[:, par, :], ln_st[:, par, :]).then_inc(s["ln_mv"], 1)

        LN_STEPS = 4

        def ln_rstd(pool, f, t, par):
            n = LN0[f] + t
            m = LN_STEPS * n

            def step(out, a, b, op):
                pool.tensor_tensor(out, a, b, op).then_inc(s["ln_ready"], 1)

            wait(pool, "ln_mv", n + 1)
            wait(pool, "xn_ready", n - 1)
            step(ln_ve[:, par, :], ln_mv[:, par, 1:2], const[:, C_EPS:C_EPS + 1], ALU.add)
            step(ln_nm[:, par, :], ln_mv[:, par, 0:1], const[:, C_NEG:C_NEG + 1], ALU.mult)
            pool.wait_ge(s["ln_ready"], m + 2)
            step(ln_rs[:, par, :], ln_ve[:, par, :], const[:, C_POW:C_POW + 1], ALU.pow)
            pool.wait_ge(s["ln_ready"], m + 3)
            step(ln_nr[:, par, :], ln_nm[:, par, :], ln_rs[:, par, :], ALU.mult)

        def ln_apply(act, f, t, par, free, free_at):
            n = LN0[f] + t
            wait(act, "ln_ready", LN_STEPS * (n + 1))
            wait(act, free, free_at)
            act.activation(xn[:, par, :], x_tile(t), ACT.Identity, bias=ln_nr[:, par, :],
                           scale=ln_rs[:, par, :]).then_inc(s["xn_ready"], 1)

        GATE_STEPS = 16

        block = ctx.enter_context(nc.Block())

        @block.sync
        def _(sp):
            def load(dst, src, name):
                sp.dma_start(dst, src).then_inc(s[name], 16)

            def col(v):
                return v.rearrange("(p o) -> p o", o=1)

            load(const[:], a["const"], "const_in")
            for L in range(2):
                for n, w in enumerate("qkvo"):
                    load(w_raw[:, L, n, :], a[f"L{L}_xattn_W{w}"], "attn_w_in")
                for n, w in enumerate("qkv"):
                    load(b_col[:, L, n:n + 1], col(a[f"L{L}_xattn_b{w}"]), "attn_w_in")
                load(bo_row[:, L, :], a[f"L{L}_xattn_bo"].partition_broadcast(P), "attn_w_in")
            load(graw[:, 0:2], a["g_xattn"].partition_broadcast(P), "g_in")
            load(graw[:, 2:4], a["g_ffn"].partition_broadcast(P), "g_in")
            for b in range(BT):
                load(m_int[b * S:(b + 1) * S, :], a["mask_1x1xSxS2_ik0"][0, 0], "mask_in")

            x_d = a["x"].rearrange("b s d -> (b s) d")
            c_d = a["ctx_1024"].rearrange("b s d -> (b s) d")
            o_d = out.rearrange("b s d -> (b s) d")

            def load_ctx(L, t, par):
                wait(sp, "xc_tr", L * T + t - 1)
                sp.dma_start(ctx_in[:, par, :], c_d[bass.ds(t * P, P), :]).then_inc(ctx_ld[par], 16)

            def attention0(t, par, has):
                if has(3):
                    if not isinstance(t, int) or t + 3 >= 2:
                        wait(sp, "ln", t + 2)
                    sp.dma_start(x_all[:, bass.ds((t + 3) * D, D)], x_d[bass.ds((t + 3) * P, P), :])\
                        .then_inc(x_in[1 - par], 16)
                if has(1):
                    load_ctx(0, t + 1, 1 - par)

            run_tiles(sp, attention0, 3, 0)

            load(gate_w[:, 0:E], a["L0_ffn_gate_w"], "moe_w_in")
            load(gate_w[:, E:GW], a["L0_ffn_dp_w1"], "moe_w_in")
            load(gate_b[:, 0:E], a["L0_ffn_gate_b"].partition_broadcast(P), "moe_w_in")
            load(gate_b[:, E:GW], a["L0_ffn_dp_b1"].partition_broadcast(P), "moe_w_in")
            load(dp_w2[:], a["L0_ffn_dp_w2"].rearrange("h o -> (h o)").partition_broadcast(P), "moe_w_in")
            load(dp_b2[:], a["L0_ffn_dp_b2"].partition_broadcast(P), "moe_w_in")
            load(ew1[:], a["L0_ffn_ew1"].rearrange("e d h -> d e h"), "moe_w_in")
            load(ew2[:], a["L0_ffn_ew2"].rearrange("e (c h) d -> h (e c) d", c=2), "moe_w_in")
            sp.dma_start(eb1[:], a["L0_ffn_eb1"].rearrange("e (c h) -> h (e c)", c=2),
                         allow_slow_non_contiguous=True).then_inc(s["moe_w_in"], 16)
            load(eb2[:], a["L0_ffn_eb2"].rearrange("e d -> (e d)").partition_broadcast(P), "moe_w_in")
            load(f_w1[:], a["L1_ffn_w1"].rearrange("(c p) d -> p c d", p=P), "ffn_w_in")
            load(f_w2[:], a["L1_ffn_w2"], "ffn_w_in")
            load(f_cw[:], a["L1_ffn_conv_w"].rearrange("(c p) o k -> p c (o k)", p=P), "ffn_w_in")
            load(f_cb[:], a["L1_ffn_conv_b"].partition_broadcast(P), "ffn_w_in")

            def attention1(t, par, has):
                if has(1):
                    load_ctx(1, t + 1, 1 - par)

            run_tiles(sp, attention1, 1, 0)

            def store(t, par, has):
                wait(sp, "x_out", t + 1)
                sp.dma_start(o_d[bass.ds(t * P, P), :], x_tile(t)).then_inc(stored, 16)

            run_tiles(sp, store, 0, 0)
            sp.wait_ge(stored, 16 * T)

        MOE_LOADS = 10

        @block.gpsimd
        def _(pool):
            pool.memset(xtap[:], 0.0).then_inc(s["ones_set"], 1)
            pool.wait_ge(s["const_in"], 16)

            def attention(L):
                def step(t, par, has):
                    if has(3):
                        ln_rstd(pool, 2 * L, t + 3, 1 - par)
                    if has(1):
                        n = L * T + t + 1
                        wait(pool, "xn_ready", L * T + t + 2)
                        pool.tensor_tensor(x_tile(t + 1), x_tile(t + 1), bo_row[:, L, :], ALU.add)\
                            .then_inc(s["bo_added"], 1)
                return step

            pool.wait_ge(s["setup_v"], 2)
            run_tiles(pool, attention(0), 3, 0)

            def experts(u, par, has):
                def add_biases(k, j):
                    t = G * (u + k) + j
                    wait(pool, "eb_mult", E * (t + 1))
                    wait(pool, "eb_added", t)
                    pool.tensor_tensor(eb_acc[:, :, :], eb_t[:, j % 2, 0:2, :], eb_t[:, j % 2, 2:4, :], ALU.add)\
                        .then_inc(s["eb_v"], 1)
                    pool.wait_ge(s["eb_v"], 2 * t + 1)
                    pool.tensor_tensor(eb_sum[:], eb_acc[:, 0, :], eb_acc[:, 1, :], ALU.add)\
                        .then_inc(s["eb_v"], 1)
                    pool.wait_ge(s["eb_v"], 2 * t + 2)
                    pool.tensor_tensor(x_tile(t), x_tile(t), eb_sum[:], ALU.add).then_inc(s["eb_added"], 1)

                if has(0):
                    add_biases(0, 2)
                    add_biases(0, 3)
                if has(1):
                    add_biases(1, 0)
                    add_biases(1, 1)
                if has(3):
                    m = 4 * (u + 3)

                    def step(out, a, b, op):
                        pool.tensor_tensor(out, a, b, op).then_inc(s["m_ready"], 1)

                    def all_tiles(c):
                        return const[:, c:c + 1].to_broadcast([P, G])

                    wait(pool, "m_mean", G * (u + 4))
                    wait(pool, "m_xn_ready", G * (u + 2))
                    step(m_ve[:, 1 - par, :], m_mv[:, 1 - par, :, 1], all_tiles(C_EPS), ALU.add)
                    step(m_nm[:, 1 - par, :], m_mv[:, 1 - par, :, 0], all_tiles(C_NEG), ALU.mult)
                    pool.wait_ge(s["m_ready"], m + 2)
                    step(m_rs[:, 1 - par, :], m_ve[:, 1 - par, :], all_tiles(C_POW), ALU.pow)
                    pool.wait_ge(s["m_ready"], m + 3)
                    step(m_nr[:, 1 - par, :], m_nm[:, 1 - par, :], m_rs[:, 1 - par, :], ALU.mult)

            run_tiles(pool, experts, 3, 0, T=NG)
            run_tiles(pool, attention(1), 3, 0)

            def ffn(t, par, has):
                if has(4):
                    ln_rstd(pool, 3, t + 4, par)

            run_tiles(pool, ffn, 4, 0, lo=4)

        @block.scalar
        def _(act):
            act.wait_ge(s["g_in"], 32)
            act.activation(tg[:], graw[:], ACT.Tanh).then_inc(s["tanh_done"], 1)
            act.wait_ge(s["tanh_done"], 1)
            for L in range(2):
                act.wait_ge(s["w_tr"], L + 1)
                act.activation(w_t[:, L, 0:3, :], bank[L][:, 0:3 * P], ACT.Copy).then_inc(s["w_copied"], 1)
                act.activation(w_t[:, L, 3, :], bank[L][:, 3 * P:], ACT.Copy, scale=tg[:, L:L + 1])\
                    .then_inc(s["w_copied"], 1)

            def attention(L):
                def step(t, par, has):
                    n = L * T + t
                    o = 1 - par
                    if has(1):
                        wait(act, "xc_tr", n + 2)
                        wait(act, "qkv_mm", n)
                        act.activation(xct[:, o, :, :, :, :].rearrange("p a b c k -> p (a b) c k"),
                                       bank[4][:, 0:2 * P].rearrange("p (a k) -> p a k", k=S).unsqueeze(2)
                                       .to_broadcast([P, 2 * BT, 2, S]), ACT.Copy).then_inc(s["xc_copied"], 1)
                    if has(-2):
                        wait(act, "o_tr", n - 1)
                        wait(act, "wo_mm", n - 2)
                        act.activation(o_t[:], bank[7][:, 0:P], ACT.Identity, bias=b_col[:, L, 2:3])\
                            .then_inc(s["o_copied"], 1)
                    if has(-1):
                        for half in range(2):
                            wait(act, "p_tr", 2 * (n - 1) + half + 1)
                            wait(act, "pv_mm", n - 1)
                            act.activation(prob_t[:, 4 * half:4 * half + 4, :], bank[2 + half][:], ACT.Copy)\
                                .then_inc(s["p_copied"], 1)
                    if has(0):
                        for half in range(2):
                            wait(act, "sub_done", 2 * n + half + 1)
                            v = prob[:, par, half * 512:(half + 1) * 512]
                            act.activation(v, v, ACT.Exp, scale=SCALE).then_inc(s["exp_done"], 1)
                    if has(2):
                        ln_apply(act, 2 * L, t + 2, par, "xc_tr", n + 1)
                return step

            run_tiles(act, attention(0), 3, 2)

            def experts(u, par, has):
                o = 1 - par

                def relu(c):
                    wait(act, "hid_mm", EC * u + c + 1)
                    if c == 0:
                        wait(act, "y_mm", G * u)
                    act.activation(hid[:, c, :], bank[c % 4][:], ACT.Relu, bias=eb1[:, c:c + 1])\
                        .then_inc(s["relu_a"], 1)

                def bias_products(k, j):
                    t = G * (u + k) + j
                    wait(act, "eb_v", 2 * (t - 2) + 1)
                    for e in range(E):
                        act.activation(eb_t[:, j % 2, e, :], eb2[:, e * P:(e + 1) * P], ACT.Copy,
                                       scale=gwt[:, o if k else par, j, e:e + 1]).then_inc(s["eb_mult"], 1)

                if has(0):
                    relu(0)
                    relu(2)
                if has(1):
                    wait(act, "mx_tr", u + 2)
                    wait(act, "gate_mm", u + 1)
                    act.activation(mxt[:], bank[4][:], ACT.Copy).then_inc(s["mx_copied"], 1)
                    wait(act, "hid_mm", EC * u)
                    act.activation(mx_hi[:, o, :], bank[4][:], ACT.Copy).then_inc(s["mx_hi_done"], 1)
                if has(0):
                    relu(4)
                    relu(6)
                if has(0):
                    bias_products(0, 2)
                    bias_products(0, 3)
                if has(1):
                    wait(act, "gate_v", GATE_STEPS * (u + 1) + 6)
                    act.activation(ge[:], gls[:], ACT.Exp).then_inc(s["exp_gate"], 1)
                if has(2):
                    wait(act, "m_ready", 4 * (u + 3))
                    wait(act, "mx_tr", u + 2)
                    for j in range(G):
                        act.activation(m_xn[:, j, :], x_tile(G * (u + 2) + j), ACT.Identity,
                                       bias=m_nr[:, par, j:j + 1], scale=m_rs[:, par, j:j + 1])\
                            .then_inc(s["m_xn_ready"], 1)
                if has(1):
                    wait(act, "gate_done", u + 2)
                    bias_products(1, 0)
                    bias_products(1, 1)

            act.wait_ge(s["moe_w_in"], 16 * MOE_LOADS)
            act.activation(ew1_hi[:].rearrange("p c h -> p (c h)"), ew1[:].rearrange("p e h -> p (e h)"), ACT.Copy)\
                .then_inc(s["ew1_split"], 1)
            run_tiles(act, experts, 2, 0, T=NG)
            run_tiles(act, attention(1), 3, 2)

            for k in range(TAPS):
                act.wait_ge(s["tap_tr"], k + 1)
                act.activation(f_wk[:, k, :], bank[k][:], ACT.Copy).then_inc(s["tap_copied"], 1)
            act.wait_ge(s["tap_tr"], TAPS + 1)
            act.activation(f_w2t[:].rearrange("p c d -> p (c d)"), bank[3][:], ACT.Copy).then_inc(s["w2t_copied"], 1)

            def ffn(t, par, has):
                o = 1 - par
                if has(-2):
                    wait(act, "sc_ready", t + 2)
                    wait(act, "q2_tr", t - 3)
                    act.activation(q2[:, par, :], hact[:, par, :], ACT.Identity, scale=sc_q[:, o, 1:2],
                                   bias=const[:, C_RND:C_RND + 1]).then_inc(s["q2_ready"], 1)
                if has(-1):
                    wait(act, "hpre_done", t)
                    wait(act, "h_max", t - 2)
                    act.activation(hact[:, o, :], hpre[:, o, :], ACT.Silu).then_inc(s["silu_done"], 1)
                if has(1):
                    wait(act, "sc_ready", t + 2)
                    wait(act, "xq_ready", t + 1)
                    act.activation(q1[:], xn[:, o, :], ACT.Identity, scale=sc_q[:, o, 0:1],
                                   bias=const[:, C_RND:C_RND + 1]).then_inc(s["q1_done"], 1)
                if has(3):
                    wait(act, "q1_done", t + 2)
                    ln_apply(act, 3, t + 3, o, "x_max", t + 2)
                if has(1):
                    wait(act, "xq_tr", t + 2)
                    wait(act, "conv_mm", t)
                    src = bank[4][:, 0:P].rearrange("p (b s) -> p b s", b=BT)
                    act.activation(xtap[:, o, 0, :, 1:S], src[:, :, 0:S - 1], ACT.Copy)
                    act.activation(xtap[:, o, 1, :, :], src, ACT.Copy)
                    act.activation(xtap[:, o, 2, :, 0:S - 1], src[:, :, 1:S], ACT.Copy).then_inc(s["xq_copied"], 1)

            run_tiles(act, ffn, 4, 2, lo=4)

        @block.vector
        def _(dve):
            dve.wait_ge(s["const_in"], 16)
            dve.tensor_copy(ident16[:], ident).then_inc(s["ident16_done"], 1)
            for par in range(2):
                for b in range(BT):
                    dve.tensor_copy(vb[:, par, :, b, :, HD:VW],
                                    const[:, C_H:C_H + 2].unsqueeze(1).unsqueeze(3).to_broadcast([P, NPAIR, 2, 1]))\
                        .then_inc(s["ones_set"], 1)
            dve.wait_ge(s["attn_w_in"], 16 * 16)
            dve.wait_ge(s["tanh_done"], 1)
            for L in range(2):
                dve.tensor_scalar(bo_row[:, L, :], bo_row[:, L, :], tg[:, L:L + 1], None, ALU.mult)\
                    .then_inc(s["setup_v"], 1)
            dve.tensor_copy(q_mask[:, 0, :, :], const[:, C_R:C_R + RQ].unsqueeze(2).to_broadcast([P, RQ, P]))\
                .then_inc(s["setup_v"], 1)
            dve.wait_ge(s["mask_in"], 32)
            dve.tensor_scalar(m_keep[:], m_int[:], 0.0, None, ALU.not_equal).then_inc(s["mask_v"], 1)
            dve.wait_ge(s["mask_v"], 1)
            dve.tensor_reduce(m_any[:], m_keep[:], AX.X, ALU.max).then_inc(s["mask_v"], 1)
            dve.wait_ge(s["mask_v"], 2)
            dve.tensor_scalar(m_dead[:], m_any[:], -1.0, 1.0, ALU.mult, ALU.add).then_inc(s["mask_v"], 1)
            dve.tensor_scalar(m_diag[:], const[0:S, C_ID:C_ID + S], m_any[0:S, :], None, ALU.mult)\
                .then_inc(s["mask_v"], 1)
            dve.wait_ge(s["mask_v"], 4)
            dve.tensor_scalar(m_keep2[:], m_keep[:], m_dead[:], 1.0, ALU.max, ALU.subtract).then_inc(s["mask_v"], 1)
            dve.wait_ge(s["mask_v"], 5)
            dve.tensor_scalar(neg_mask[:], m_keep2[:], NEG, None, ALU.mult).then_inc(s["mask_v"], 1)
            dve.wait_ge(s["alive_mm"], 1)
            for r in range(RQ):
                dve.tensor_scalar(q_mask[:, 1, r, :].rearrange("p (b s) -> p b s", b=BT),
                                  bank[6][:, 0:S].unsqueeze(1).to_broadcast([P, BT, S]),
                                  const[:, C_R + r:C_R + r + 1], None, ALU.mult).then_inc(s["setup_v"], 1)

            def attention(L):
                def step(t, par, has):
                    n = L * T + t
                    o = 1 - par
                    if has(-2):
                        wait(dve, "pv_mm", n - 1)
                        wait(dve, "o_tr", n - 3)
                        ov = bank[6][:, 0:NPAIR * BT * 2 * VW].rearrange("p (i b h v) -> p i b h v", i=NPAIR, b=BT, h=2)
                        rv = rden[:].rearrange("p (i h) -> p i h", h=2)
                        onv = o_n[:, par, :].rearrange("p (i h v) -> p i h v", i=NPAIR, h=2)
                        wait(dve, "o_norm", 2 * (n - 2))
                        for b in range(BT):
                            q = slice(b * S, (b + 1) * S)
                            dve.reciprocal(rv[q], ov[q, :, b, :, HD]).then_inc(s["rden_done"], 1)
                    if has(0):
                        wait(dve, "pv_mm", n - 1)
                        wait(dve, "qkv_mm", n + 1)
                        for b in range(BT):
                            dve.tensor_tensor(
                                vb[:, par, :, b, :, 0:HD],
                                bank[5][:, (2 + b) * P:(3 + b) * P].rearrange("p (i h v) -> p i h v", i=NPAIR, h=2),
                                const[:, C_H:C_H + 2].unsqueeze(1).unsqueeze(3).to_broadcast([P, NPAIR, 2, HD]),
                                ALU.mult).then_inc(s["v_ready"], 1)
                    if has(-2):
                        dve.wait_ge(s["rden_done"], 2 * (n - 1))
                        for b in range(BT):
                            q = slice(b * S, (b + 1) * S)
                            dve.tensor_tensor(onv[q], ov[q, :, b, :, 0:HD],
                                              rv[q].unsqueeze(3).to_broadcast([S, NPAIR, 2, HD]), ALU.mult)\
                                .then_inc(s["o_norm"], 1)
                    if has(0):
                        for half in range(2):
                            wait(dve, "scores_mm", 2 * n + half + 1)
                            sc = bank[half][:].rearrange("p (h k) -> p h k", k=S)
                            m = smax[:, half * 8:half * 8 + 8]
                            wait(dve, "sub_done", 2 * n + half - 1)
                            dve.tensor_reduce(m, sc, AX.X, ALU.max).then_inc(s["smax_done"], 1)
                            dve.wait_ge(s["smax_done"], 2 * n + half + 1)
                            wait(dve, "p_tr", 2 * (n - 1))
                            dve.tensor_tensor(prob[:, par, half * 512:(half + 1) * 512].rearrange("p (h k) -> p h k", k=S),
                                              sc, m.unsqueeze(2).to_broadcast([P, 8, S]), ALU.subtract)\
                                .then_inc(s["sub_done"], 1)
                    if has(3):
                        ln_stats(dve, 2 * L, t + 3, o)
                        ln_mean_ready(dve, 2 * L, t + 3)
                    if has(1):
                        wait(dve, "qkv_mm", n + 2)
                        wait(dve, "scores_mm", 2 * n)
                        dve.scalar_tensor_tensor(
                            out=qq[:, o, :, :], in0=bank[5][:, 0:P].unsqueeze(1).to_broadcast([P, RQ, P]),
                            scalar=b_col[:, L, 0:1], in1=q_mask[:, L, :, :], op0=ALU.add, op1=ALU.mult)\
                            .then_inc(s["qk_ready"], 1)
                        dve.scalar_tensor_tensor(
                            out=kj[:, o, :, :], in0=bank[5][:, P:2 * P].unsqueeze(1).to_broadcast([P, JH, P]),
                            scalar=b_col[:, L, 1:2],
                            in1=const[:, C_J:C_J + JH].unsqueeze(2).to_broadcast([P, JH, P]),
                            op0=ALU.add, op1=ALU.mult).then_inc(s["qk_ready"], 1)
                    if has(3):
                        ln_mean(dve, o)
                    if has(-2):
                        wait(dve, "wo_mm", n - 1)
                        wait(dve, "bo_added", n - 1)
                        dve.tensor_tensor(x_tile(t - 2), bank[7][:, P:2 * P], x_tile(t - 2), ALU.add)\
                            .then_inc(s["x_attn"], 1)
                return step

            run_tiles(dve, attention(0), 3, 2, lo=4)

            dve.wait_ge(s["moe_w_in"], 16 * MOE_LOADS)
            dve.tensor_scalar(thr[:], const[:, C_THR:C_THR + E - 1], dp_b2[:], None, ALU.subtract)\
                .then_inc(s["setup_v"], 1)
            dve.wait_ge(s["setup_v"], 8)
            dve.wait_ge(s["ew1_split"], 1)
            dve.tensor_tensor(ew1_lo[:].rearrange("p c h -> p (c h)"), ew1[:].rearrange("p e h -> p (e h)"),
                              ew1_hi[:].rearrange("p c h -> p (c h)"), ALU.subtract).then_inc(s["ew1_split"], 1)

            def experts(u, par, has):
                o = 1 - par
                m0 = GATE_STEPS * (u + 1)
                lg = gl[:, :, 0:E]

                def gate(k, ins):
                    ins.then_inc(s["gate_v"], 1)

                def after(k):
                    dve.wait_ge(s["gate_v"], m0 + k)

                def relu(c):
                    wait(dve, "hid_mm", EC * u + c + 1)
                    if c == 1:
                        wait(dve, "y_mm", G * u)
                    dve.tensor_scalar(hid[:, c, :], bank[c % 4][:], eb1[:, c:c + 1], 0.0, ALU.add, ALU.max)\
                        .then_inc(s["relu_v"], 1)

                def combine(j, e):
                    t = G * u + j
                    src = x_tile(t) if e == 0 else y_acc[:, (e - 1) % 2, :]
                    dst = x_tile(t) if e == E - 1 else y_acc[:, e % 2, :]
                    if e == 0:
                        wait(dve, "y_mm", t + 1)
                        wait(dve, "eb_added", t + 1)
                    wait(dve, "y_v", E * t + e)
                    dve.scalar_tensor_tensor(out=dst, in0=bank[6 + j % 2][:, e * P:(e + 1) * P],
                                             scalar=gwt[:, par, j, e:e + 1], in1=src, op0=ALU.mult, op1=ALU.add)\
                        .then_inc(s["y_v"], 1)

                def per_tile(v, n):
                    return v[:].unsqueeze(2).to_broadcast([P, G, n])

                if has(0):
                    relu(1)
                    relu(3)
                if has(1):
                    wait(dve, "mx_hi_done", u + 2)
                    wait(dve, "hid_mm", EC * u)
                    dve.tensor_tensor(mx_lo[:, o, :], bank[4][:], mx_hi[:, o, :], ALU.subtract)\
                        .then_inc(s["mx_lo_done"], 1)
                if has(0):
                    relu(5)
                if has(0):
                    relu(7)
                if has(1):
                    wait(dve, "gate_mm", u + 2)
                    wait(dve, "gate_done", u + 1)
                    gate(1, dve.tensor_tensor(gl[:], bank[5][:, 0:G * GW].rearrange("p (g w) -> p g w", g=G),
                                              gate_b[:].unsqueeze(1).to_broadcast([P, G, GW]), ALU.add))
                    after(1)
                    gate(2, dve.scalar_tensor_tensor(out=gj[:], in0=gl[:, :, E:GW], scalar=0.0,
                                                     in1=dp_w2[:].unsqueeze(1).to_broadcast([P, G, DPH]),
                                                     op0=ALU.max, op1=ALU.mult))
                    gate(3, dve.tensor_reduce(gm[:], lg, AX.X, ALU.max))
                    l_row = lg.unsqueeze(2).to_broadcast([P, G, E, E])
                    l_col = lg.unsqueeze(3).to_broadcast([P, G, E, E])
                    tie = const[:, C_TIE:C_TIE + E * E].unsqueeze(1).to_broadcast([P, G, E * E])
                    gate(4, dve.tensor_tensor(g_gt[:], l_row, l_col, ALU.is_gt))
                    gate(5, dve.tensor_tensor(g_eq[:], l_row, l_col, ALU.is_equal))
                    after(3)
                    wait(dve, "exp_gate", u + 1)
                    gate(6, dve.tensor_tensor(gls[:], lg, per_tile(gm, E), ALU.subtract))
                    after(5)
                    eq = g_eq[:].rearrange("p g e f -> p g (e f)")
                    gate(7, dve.tensor_tensor(eq, eq, tie, ALU.mult))
                    gate(8, dve.tensor_reduce(gz[:], gj[:], AX.X, ALU.add))
                    after(7)
                    gate(9, dve.tensor_tensor(g_gt[:], g_gt[:], g_eq[:], ALU.add))
                    after(8)
                    gate(10, dve.tensor_tensor(gs3[:], thr[:].unsqueeze(1).to_broadcast([P, G, E - 1]),
                                               per_tile(gz, E - 1), ALU.is_le))
                if has(0):
                    combine(0, 0)
                if has(1):
                    after(9)
                    gate(11, dve.tensor_reduce(g_rank[:], g_gt[:], AX.X, ALU.add))
                    after(10)
                    gate(12, dve.tensor_reduce(gk[:], gs3[:], AX.X, ALU.add))
                if has(0):
                    combine(0, 1)
                if has(1):
                    after(12)
                    gate(13, dve.tensor_tensor(g_sel[:], g_rank[:], per_tile(gk, E), ALU.is_le))
                if has(0):
                    combine(0, 2)
                if has(1):
                    after(13)
                    wait(dve, "exp_gate", u + 2)
                    gate(14, dve.tensor_tensor(g_ew[:], g_sel[:], ge[:], ALU.mult))
                if has(0):
                    combine(0, 3)
                if has(1):
                    after(14)
                    gate(15, dve.tensor_reduce(g_sum[:], g_ew[:], AX.X, ALU.add))
                if has(0):
                    combine(1, 0)
                if has(1):
                    after(15)
                    gate(16, dve.reciprocal(g_rs[:], g_sum[:]))
                if has(0):
                    combine(1, 1)
                if has(1):
                    after(16)
                    wait(dve, "y_v", E * G * u)
                    wait(dve, "eb_mult", E * G * u)
                    dve.scalar_tensor_tensor(out=gwt[:, o, :, :], in0=g_ew[:], scalar=tg[:, 2:3],
                                             in1=per_tile(g_rs, E), op0=ALU.mult, op1=ALU.mult)\
                        .then_inc(s["gate_done"], 1)
                if has(0):
                    combine(1, 2)
                    combine(1, 3)
                if has(3):
                    for j in range(G):
                        wait(dve, "x_attn", G * (u + 3) + j + 1)
                        if j == 0:
                            wait(dve, "m_mean", G * (u + 2))
                        dve.bn_stats(m_st[:, o, j, :], x_tile(G * (u + 3) + j)).then_inc(s["m_ln"], 1)
                if has(0):
                    for e in range(E):
                        combine(2, e)
                if has(3):
                    wait(dve, "m_ready", 4 * (u + 2))
                    wait(dve, "m_ln", G * (u + 4))
                if has(0):
                    combine(3, 0)
                if has(3):
                    for j in range(G):
                        dve.bn_aggr(m_mv[:, o, j, :], m_st[:, o, j, :]).then_inc(s["m_mean"], 1)
                if has(0):
                    for e in range(1, E):
                        combine(3, e)

            run_tiles(dve, experts, 3, 0, T=NG)
            run_tiles(dve, attention(1), 3, 2, lo=4)

            dve.wait_ge(s["ffn_w_in"], 64)
            dve.tensor_reduce(f_s[:, 0:1], f_w1[:].rearrange("p c d -> p (c d)"), AX.X, ALU.add,
                              apply_absolute_value=True).then_inc(s["ffn_sum"], 1)
            dve.tensor_reduce(f_s[:, 1:2], f_w2[:], AX.X, ALU.add, apply_absolute_value=True)\
                .then_inc(s["ffn_sum"], 1)
            dve.wait_ge(s["sum_mm"], 1)
            k = [0]

            def tern(ins):
                k[0] += 1
                ins.then_inc(s["tern"], 1)
                dve.wait_ge(s["tern"], k[0])

            tern(dve.tensor_scalar(f_s[:, 2:4], bank[6][:, 0:2], 1.0 / (F * D), Q_EPS, ALU.mult, ALU.max))
            tern(dve.reciprocal(f_s[:, 4:6], f_s[:, 2:4]))
            for w, i in ((f_w1[:].rearrange("p c d -> p (c d)"), 0), (f_w2[:], 1)):
                tern(dve.tensor_scalar(w, w, f_s[:, 4 + i:5 + i], ROUND, ALU.mult, ALU.add))
                tern(dve.tensor_scalar(w, w, ROUND, 1.0, ALU.subtract, ALU.min))
                tern(dve.tensor_scalar(w, w, -1.0, None, ALU.max))
            tern(dve.tensor_scalar(f_cw[:], f_cw[:], f_s[:, 2:3], None, ALU.mult))
            tern(dve.tensor_scalar(f_s[:, 6:7], f_s[:, 3:4], tg[:, 3:4], 1.0 / 127.0, ALU.mult, ALU.mult))
            for tap in range(TAPS):
                for c in range(FC):
                    dve.tensor_scalar(f_tap[:, tap, c, :], f_w1[:, c, :], f_cw[:, c, tap:tap + 1], None, ALU.mult)\
                        .then_inc(s["tap_ready"], 1)

            dve.tensor_scalar(sc_f[:, 0:1], ones[:, 0:1], 1.0 / 127.0, None, ALU.mult).then_inc(s["sc_set"], 1)
            dve.tensor_scalar(sc_f[:, 1:2], f_s[:, 6:7], 1.0, None, ALU.mult).then_inc(s["sc_set"], 1)
            dve.tensor_scalar(sc_m[:], ones[:, 0:2], 1.0, None, ALU.mult).then_inc(s["sc_set"], 1)
            dve.wait_ge(s["sc_set"], 3)

            def ffn(t, par, has):
                o = 1 - par
                scales = has(2) or has(-1)
                if has(-3):
                    wait(dve, "q2_tr", t - 2)
                    wait(dve, "out_mm", t - 4)
                    dve.tensor_scalar(q2t[:, o, :], bank[5][:], ROUND, 127.0, ALU.subtract, ALU.min)\
                        .then_inc(s["q2_copied"], 1)
                if has(-4):
                    wait(dve, "out_mm", t - 3)
                    wait(dve, "sc_late", t - 3)
                    dve.scalar_tensor_tensor(out=x_tile(t - 4), in0=bank[6][:, 0:P], scalar=sc_l[:],
                                             in1=x_tile(t - 4), op0=ALU.mult, op1=ALU.add).then_inc(s["x_out"], 1)
                if has(4):
                    ln_stats(dve, 3, t + 4, par)
                if has(2):
                    wait(dve, "xn_ready", 2 * T + t + 3)
                    wait(dve, "sc_v", 2 * (t + 2))
                    dve.tensor_reduce(sc_m[:, 0:1], xn[:, par, :], AX.X, ALU.max, apply_absolute_value=True)\
                        .then_inc(s["x_max"], 1)
                if has(-1):
                    wait(dve, "silu_done", t)
                    dve.tensor_reduce(sc_m[:, 1:2], hact[:, o, :], AX.X, ALU.max, apply_absolute_value=True)\
                        .then_inc(s["h_max"], 1)
                if has(4):
                    ln_mean_ready(dve, 3, t + 4)
                if has(1):
                    wait(dve, "q1_done", t + 2)
                    wait(dve, "xq_tr", t)
                    dve.tensor_scalar(xdq[:, o, :], q1[:], ROUND, sc_i[:, o, 0:1], ALU.subtract, ALU.mult)\
                        .then_inc(s["xq_ready"], 1)
                if scales:
                    if has(2):
                        wait(dve, "x_max", t + 3)
                    if has(-1):
                        wait(dve, "h_max", t)
                    wait(dve, "sc_ready", t + 2)
                    dve.tensor_scalar(sc_c[:], sc_m[:], Q_EPS, None, ALU.max).then_inc(s["sc_v"], 1)
                if has(4):
                    ln_mean(dve, par)
                if has(-3):
                    wait(dve, "x_out", t - 3)
                    dve.tensor_scalar(sc_l[:], sc_i[:, par, 1:2], 1.0, None, ALU.mult).then_inc(s["sc_late"], 1)
                if scales:
                    dve.wait_ge(s["sc_v"], 2 * (t + 2) + 1)
                    dve.reciprocal(sc_r[:], sc_c[:]).then_inc(s["sc_v"], 1)
                    if has(0):
                        wait(dve, "xq_ready", t + 1)
                    if has(-3):
                        wait(dve, "sc_late", t - 2)
                    dve.tensor_tensor(sc_i[:, par, :], sc_c[:], sc_f[:], ALU.mult)
                if has(0):
                    wait(dve, "conv_mm", t + 1)
                    wait(dve, "silu_done", t - 1)
                    dve.tensor_tensor(hpre[:, par, :], bank[par][:], f_cb[:], ALU.add).then_inc(s["hpre_done"], 1)
                if scales:
                    dve.wait_ge(s["sc_v"], 2 * (t + 2) + 2)
                    if has(0):
                        wait(dve, "q1_done", t + 1)
                    if has(-3):
                        wait(dve, "q2_ready", t - 2)
                    dve.tensor_scalar(sc_q[:, par, :], sc_r[:], 127.0, None, ALU.mult).then_inc(s["sc_ready"], 1)

            run_tiles(dve, ffn, 4, 4, lo=4)

        @block.tensor
        def _(pe):
            def tr(dst, src):
                return pe.transpose(dst, src, ident)

            pe.wait_ge(s["const_in"], 16)
            pe.wait_ge(s["attn_w_in"], 16 * 16)
            for L in range(2):
                for n in range(4):
                    last = tr(bank[L][:, n * P:(n + 1) * P], w_raw[:, L, n, :])
                last.then_inc(s["w_tr"], 1)
            pe.wait_ge(s["mask_v"], 4)
            pe.matmul(bank[6][:, 0:S], ones[0:S, :], m_diag[:], start=True, stop=True).then_inc(s["alive_mm"], 1)
            pe.wait_ge(s["w_copied"], 4)
            pe.wait_ge(s["setup_v"], 7)
            pe.wait_ge(s["mask_v"], 6)
            pe.wait_ge(s["ident16_done"], 1)
            pe.wait_ge(s["ones_set"], 5)

            def attention(L):
                def step(t, par, has):
                    n = L * T + t
                    o = 1 - par
                    if has(0):
                        wait(pe, "qk_ready", 2 * n + 2)
                        for half in range(2):
                            wait(pe, "sub_done", 2 * n + half - 1)
                            if L == 1:
                                pe.matmul(bank[half][:].rearrange("p (h k) -> p h k", k=S), ident16[:],
                                          neg_mask[:].unsqueeze(1).to_broadcast([P, 8, S]),
                                          start=True, stop=False, skip_group_check=True)
                            for rr in range(2):
                                r = half * 2 + rr
                                for b in range(BT):
                                    q = slice(b * S, (b + 1) * S)
                                    last = pe.matmul(bank[half][q, rr * 256:(rr + 1) * 256], qq[:, par, r, q],
                                                     kj[:, par, :, q], start=(L == 0), stop=True,
                                                     skip_group_check=True)
                            last.then_inc(s["scores_mm"], 1)
                    if has(1):
                        wait(pe, "xn_ready", L * T + t + 2)
                        wait(pe, "xc_copied", n + 1)
                        tr(bank[4][:, 0:P], xn[:, o, :])
                        pe.wait_ge(ctx_ld[o], L * T * 8 + (t + 1 + 1 + par) * 8)
                        tr(bank[4][:, P:2 * P], ctx_in[:, o, :]).then_inc(s["xc_tr"], 1)
                    if has(-2):
                        wait(pe, "o_norm", 2 * (n - 1))
                        wait(pe, "x_attn", n - 2)
                        tr(bank[7][:, 0:P], o_n[:, par, :]).then_inc(s["o_tr"], 1)
                    if has(-1):
                        for half in range(2):
                            wait(pe, "exp_done", 2 * (n - 1) + half + 1)
                            wait(pe, "p_copied", 2 * (n - 2) + half + 1)
                            for i in range(4):
                                c = (half * 4 + i) * P
                                last = tr(bank[2 + half][:, i * P:(i + 1) * P], prob[:, o, c:c + P])
                            last.then_inc(s["p_tr"], 1)
                    if has(1):
                        wait(pe, "xc_copied", n + 2)
                        wait(pe, "qk_ready", 2 * n + 2)
                        wait(pe, "v_ready", 2 * n + 2)
                        pe.matmul(bank[5][:, 0:P], w_t[:, L, 0, :], xct[:, o, 0, :, 0, :], start=True, stop=True)
                        pe.matmul(bank[5][:, P:2 * P], w_t[:, L, 1, :], xct[:, o, 1, :, 0, :], start=True, stop=True)
                        for b in range(BT):
                            keys = xct[:, o, 1, b, :, :].rearrange("p c k -> p (c k)")
                            last = pe.matmul(bank[5][:, (2 + b) * P:(3 + b) * P], keys, w_t[:, L, 2, :],
                                             start=True, stop=True)
                        last.then_inc(s["qkv_mm"], 1)
                    if has(-2):
                        wait(pe, "o_copied", n - 1)
                        pe.matmul(bank[7][:, P:2 * P], o_t[:], w_t[:, L, 3, :], start=True, stop=True)\
                            .then_inc(s["wo_mm"], 1)
                    if has(-1):
                        wait(pe, "p_copied", 2 * n)
                        wait(pe, "v_ready", 2 * n)
                        wait(pe, "o_norm", 2 * (n - 1))
                        for i in range(NPAIR):
                            w = BT * 2 * VW
                            last = pe.matmul(bank[6][:, i * w:(i + 1) * w], prob_t[:, i, :],
                                             vb[:, o, i, :, :, :].rearrange("p b h v -> p (b h v)"),
                                             start=True, stop=True)
                        last.then_inc(s["pv_mm"], 1)
                return step

            run_tiles(pe, attention(0), 3, 2)

            def experts(u, par, has):
                o = 1 - par

                def hidden(c):
                    k = EC * u + c - 4
                    if c == 0:
                        wait(pe, "mx_hi_done", u + 1)
                        wait(pe, "mx_lo_done", u + 1)
                    wait(pe, "relu_a" if c % 2 == 0 else "relu_v", EC // 2 * u + (c - 4) // 2 + 1)
                    hi, lo = mx_hi[:, par, :], mx_lo[:, par, :]
                    pe.matmul(bank[c % 4][:], ew1_hi[:, c, :], hi, start=True, stop=False)
                    pe.matmul(bank[c % 4][:], ew1_hi[:, c, :], lo, start=False, stop=False)
                    pe.matmul(bank[c % 4][:], ew1_lo[:, c, :], hi, start=False, stop=True).then_inc(s["hid_mm"], 1)

                if has(0):
                    for c in range(4):
                        hidden(c)
                if has(1):
                    wait(pe, "m_xn_ready", G * (u + 2))
                    wait(pe, "mx_copied", u + 1)
                    wait(pe, "mx_lo_done", u + 1)
                    for j in range(G):
                        last = tr(bank[4][:, j * P:(j + 1) * P], m_xn[:, j, :])
                    last.then_inc(s["mx_tr"], 1)
                if has(0):
                    for c in range(4, EC):
                        hidden(c)
                if has(1):
                    wait(pe, "mx_copied", u + 2)
                    wait(pe, "gate_v", GATE_STEPS * u + 1)
                    for j in range(G):
                        last = pe.matmul(bank[5][:, j * GW:(j + 1) * GW], mxt[:, j * P:(j + 1) * P], gate_w[:],
                                         start=True, stop=True)
                    last.then_inc(s["gate_mm"], 1)
                if has(0):
                    wait(pe, "relu_a", EC // 2 * (u + 1))
                    wait(pe, "relu_v", EC // 2 * (u + 1))
                    for j in range(G):
                        wait(pe, "y_v", E * (G * u + j - 1))
                        for e in range(E):
                            for c in range(2):
                                last = pe.matmul(bank[6 + j % 2][:, e * P:(e + 1) * P],
                                                 hid[:, 2 * e + c, j * P:(j + 1) * P], ew2[:, 2 * e + c, :],
                                                 start=(c == 0), stop=(c == 1))
                        last.then_inc(s["y_mm"], 1)

            pe.wait_ge(s["x_attn"], T)
            pe.wait_ge(s["ew1_split"], 2)
            run_tiles(pe, experts, 2, 0, T=NG)
            pe.wait_ge(s["y_v"], E * T)
            run_tiles(pe, attention(1), 3, 2)
            pe.wait_ge(s["x_attn"], 2 * T)

            pe.wait_ge(s["ffn_sum"], 2)
            pe.matmul(bank[6][:, 0:2], ones, f_s[:, 0:2], start=True, stop=True).then_inc(s["sum_mm"], 1)
            for tap in range(TAPS):
                pe.wait_ge(s["tap_ready"], FC * (tap + 1))
                for c in range(FC):
                    last = tr(bank[tap][:, c * P:(c + 1) * P], f_tap[:, tap, c, :])
                last.then_inc(s["tap_tr"], 1)
            for c in range(FC):
                last = tr(bank[3][:, c * P:(c + 1) * P], f_w2[:, c * P:(c + 1) * P])
            last.then_inc(s["tap_tr"], 1)
            pe.wait_ge(s["tap_copied"], TAPS)
            pe.wait_ge(s["w2t_copied"], 1)

            def ffn(t, par, has):
                o = 1 - par
                if has(0):
                    wait(pe, "xq_copied", t + 1)
                    wait(pe, "hpre_done", t - 1)
                    for tap in range(TAPS):
                        last = pe.matmul(bank[par][:], xtap[:, par, tap, :, :].rearrange("p b s -> p (b s)"), f_wk[:, tap, :],
                                         start=(tap == 0), stop=(tap == TAPS - 1))
                    last.then_inc(s["conv_mm"], 1)
                if has(1):
                    wait(pe, "xq_ready", t + 2)
                    wait(pe, "xq_copied", t + 1)
                    tr(bank[4][:, 0:P], xdq[:, o, :]).then_inc(s["xq_tr"], 1)
                if has(-3):
                    wait(pe, "q2_copied", t - 2)
                    wait(pe, "x_out", t - 3)
                    for c in range(FC):
                        last = pe.matmul(bank[6][:, 0:P], q2t[:, o, c * P:(c + 1) * P], f_w2t[:, c, :],
                                         start=(c == 0), stop=(c == FC - 1))
                    last.then_inc(s["out_mm"], 1)
                if has(-2):
                    wait(pe, "q2_ready", t - 1)
                    wait(pe, "q2_copied", t - 2)
                    for c in range(FC):
                        last = tr(bank[5][:, c * P:(c + 1) * P], q2[:, par, c * P:(c + 1) * P])
                    last.then_inc(s["q2_tr"], 1)

            run_tiles(pe, ffn, 4, 4, lo=4)


def constants(np):
    c = np.zeros((P, C_ALL), np.float32)
    p = np.arange(P)
    c[:, C_ID:C_ID + P] = np.eye(P)
    c[:, C_ONE:C_ONE + P] = 1
    for j in range(JH):
        c[:, C_J + j] = (p // HD) % JH == j
    for r in range(RQ):
        c[:, C_R + r] = p // (JH * HD) == r
    for h in range(2):
        c[:, C_H + h] = p // S == h
    for e in range(E):
        for f in range(E):
            c[:, C_TIE + e * E + f] = f < e
    for i, v in enumerate((0.75, 1.25, 1.75)):
        z = np.float32(math.log(math.expm1(v)))
        c[:, C_THR + i] = np.nextafter(z, np.float32(2)) if i == 1 else z
    c[:, C_POW] = -0.5
    c[:, C_RND] = ROUND
    c[:, C_EPS] = LN_EPS
    c[:, C_NEG] = -1
    return c


_INS = ['x', 'ctx_1024', 'mask_1x1xSxS2_ik0', 'g_xattn', 'g_ffn'] + [
    f"L{L}_xattn_{w}{c}" for L in range(2) for c in "qkvo" for w in "Wb"] + [
    f"L0_ffn_{n}" for n in ("gate_w", "gate_b", "dp_w1", "dp_b1", "dp_w2", "dp_b2", "ew1", "eb1", "ew2", "eb2")] + [
    f"L1_ffn_{n}" for n in ("w1", "conv_w", "conv_b", "w2")]


def kernel(**inputs):
    import numpy as np
    import concourse.bacc as bacc
    from concourse.bass_utils import run_bass_kernel_spmd

    nc = bacc.Bacc("TRN2", target_bir_lowering=False, num_devices=1)
    arrays, aps = {}, {}
    for name in _INS:
        v = np.ascontiguousarray(inputs[name])
        arrays[f"in_{name}"] = v
        aps[name] = nc.dram_tensor(f"in_{name}", v.shape, mybir.dt.from_np(v.dtype), kind="ExternalInput").ap()
    arrays["in_const"] = constants(np)
    aps["const"] = nc.dram_tensor("in_const", (P, C_ALL), F32, kind="ExternalInput").ap()
    out = nc.dram_tensor("out_x", (B, S, D), F32, kind="ExternalOutput").ap()
    build(nc, aps, out)
    r = run_bass_kernel_spmd(nc, [arrays], core_ids=[0])
    return r.results[0]["out_x"]
```

```python
import math

import concourse.bass as bass
from concourse import mybir
from contextlib import ExitStack

F32 = mybir.dt.float32
BF16 = mybir.dt.bfloat16
F32R = mybir.dt.float32r
I32 = mybir.dt.int32
ALU = mybir.AluOpType
ACT = mybir.ActivationFunctionType
AX = mybir.AxisListType

P = 128
B, S, D = 128, 64, 128
H, HD = 16, 8
BT = P // S
T = B // BT
NPAIR = H // 2
JH, RQ = 4, 4
E, HE = 4, 256
EC = E * HE // P
DPH = 64
G = 4
NG = T // G
GW = E + DPH
F = 512
FC = F // P
TAPS = 3
VW = HD + 1
LN_EPS = 1e-5
Q_EPS = 1e-5
SCALE = 1.0 / math.sqrt(HD)
NEG = 1e30
ROUND = 1.5 * 2.0 ** 23

C_ID, C_ONE, C_J, C_R, C_H, C_TIE, C_THR, C_POW, C_RND, C_EPS, C_NEG = \
    0, 128, 256, 260, 264, 266, 282, 285, 286, 287, 288
C_ALL = 289


def build(nc, a, out):
    with ExitStack() as ctx:
        def sb(name, shape, dt=F32):
            return ctx.enter_context(nc.sbuf_tensor(name, shape, dt))

        def sem(name):
            return ctx.enter_context(nc.semaphore(name))

        bank = [ctx.enter_context(nc.psum_tensor(f"bank{i}", [P, 512], F32)) for i in range(8)]

        const = sb("const", [P, C_ALL])
        ident = const[:, C_ID:C_ID + P]
        ones = const[:, C_ONE:C_ONE + P]
        ident16 = sb("ident16", [P, P], BF16)
        x_all = sb("x_all", [P, T * D])
        tg = sb("tg", [P, 4])
        graw = sb("graw", [P, 4])

        w_raw = sb("w_raw", [P, 2, 4, P])
        w_t = sb("w_t", [P, 2, 4, P])
        b_col = sb("b_col", [P, 2, 3])
        bo_row = sb("bo_row", [P, 2, P])
        q_mask = sb("q_mask", [P, 2, RQ, P])
        neg_mask = sb("neg_mask", [P, S], BF16)
        m_int = sb("m_int", [P, S], I32)
        m_keep = sb("m_keep", [P, S])
        m_any = sb("m_any", [P, 1])
        m_dead = sb("m_dead", [P, 1])
        m_keep2 = sb("m_keep2", [P, S])
        m_diag = sb("m_diag", [S, S])

        gate_w = sb("gate_w", [P, GW])
        gate_b = sb("gate_b", [P, GW])
        dp_w2 = sb("dp_w2", [P, DPH])
        dp_b2 = sb("dp_b2", [P, 1])
        thr = sb("thr", [P, E - 1])
        ew1 = sb("ew1", [P, E, HE])
        eb1 = sb("eb1", [P, EC])
        ew2 = sb("ew2", [P, EC, P])
        eb2 = sb("eb2", [P, E * P])

        f_w1 = sb("f_w1", [P, FC, D])
        f_w2 = sb("f_w2", [P, F])
        f_cw = sb("f_cw", [P, FC, TAPS])
        f_cb = sb("f_cb", [P, F])
        f_tap = sb("f_tap", [P, TAPS, FC, D])
        f_wk_hi = sb("f_wk_hi", [P, TAPS, F], F32R)
        f_wk_lo = sb("f_wk_lo", [P, TAPS, F], F32R)
        f_w2t = sb("f_w2t", [P, FC, D], BF16)
        f_s = sb("f_s", [P, 8])

        ln_st = sb("ln_st", [P, 2, 6])
        ln_mv = sb("ln_mv", [P, 2, 2])
        ln_ve = sb("ln_ve", [P, 2, 1])
        ln_nm = sb("ln_nm", [P, 2, 1])
        ln_rs = sb("ln_rs", [P, 2, 1])
        ln_nr = sb("ln_nr", [P, 2, 1])
        xn = sb("xn", [P, 2, D])

        ctx_in = sb("ctx_in", [P, 2, D])
        xct = sb("xct", [P, 2, 2, BT, 2, S])
        qq = sb("qq", [P, 2, RQ, P])
        kj = sb("kj", [P, 2, JH, P])
        vb = sb("vb", [P, 2, NPAIR, BT, 2, VW])
        smax = sb("smax", [P, H])
        prob = sb("prob", [P, 2, H * S])
        prob_t = sb("prob_t", [P, NPAIR, P])
        rden = sb("rden", [P, H])
        o_n = sb("o_n", [P, 2, P])
        o_t = sb("o_t", [P, P])

        m_st = sb("m_st", [P, 2, G, 6])
        m_mv = sb("m_mv", [P, 2, G, 2])
        m_ve = sb("m_ve", [P, 2, G])
        m_nm = sb("m_nm", [P, 2, G])
        m_rs = sb("m_rs", [P, 2, G])
        m_nr = sb("m_nr", [P, 2, G])
        m_xn = sb("m_xn", [P, G, D])
        mxt = sb("mxt", [P, G * P])
        mx_hi = sb("mx_hi", [P, 2, G * P], F32R)
        mx_lo = sb("mx_lo", [P, 2, G * P], F32R)
        ew1_hi = sb("ew1_hi", [P, EC, P], F32R)
        ew1_lo = sb("ew1_lo", [P, EC, P], F32R)
        hid = sb("hid", [P, EC, G * P])
        gl = sb("gl", [P, G, GW])
        gj = sb("gj", [P, G, DPH])
        gz = sb("gz", [P, G])
        gk = sb("gk", [P, G])
        gs3 = sb("gs3", [P, G, E - 1])
        gm = sb("gm", [P, G])
        gls = sb("gls", [P, G, E])
        ge = sb("ge", [P, G, E])
        g_gt = sb("g_gt", [P, G, E, E])
        g_eq = sb("g_eq", [P, G, E, E])
        g_rank = sb("g_rank", [P, G, E])
        g_sel = sb("g_sel", [P, G, E])
        g_ew = sb("g_ew", [P, G, E])
        g_sum = sb("g_sum", [P, G])
        g_rs = sb("g_rs", [P, G])
        gwt = sb("gwt", [P, 2, G, E])
        eb_t = sb("eb_t", [P, 2, E, P])
        eb_acc = sb("eb_acc", [P, 2, P])
        eb_sum = sb("eb_sum", [P, P])
        y_acc = sb("y_acc", [P, 2, P])

        sc_m = sb("sc_m", [P, 2])
        sc_c = sb("sc_c", [P, 2])
        sc_r = sb("sc_r", [P, 2])
        sc_q = sb("sc_q", [P, 2, 2])
        sc_i = sb("sc_i", [P, 2, 2])
        sc_l = sb("sc_l", [P, 1])
        sc_f = sb("sc_f", [P, 2])
        q1 = sb("q1", [P, D])
        xdq = sb("xdq", [P, 2, D])
        x_t = sb("x_t", [P, 2, P])
        x_lo = sb("x_lo", [P, P])
        tap_hi = sb("tap_hi", [P, 2, TAPS, BT, S], F32R)
        tap_lo = sb("tap_lo", [P, 2, TAPS, BT, S], F32R)
        hpre = sb("hpre", [P, 2, F])
        hact = sb("hact", [P, 2, F])
        q2 = sb("q2", [P, 2, F])
        q2t = sb("q2t", [P, 2, F], BF16)

        names = """const_in attn_w_in moe_w_in ffn_w_in g_in mask_in
            tanh_done ident16_done w_tr w_copied setup_v mask_v alive_mm ones_set thr_done zero_set edges_set
            sum_mm ffn_sum tern tap_ready tap_tr tap_copied tap_split w2t_copied
            ln ln_mv ln_ready xn_ready
            xc_tr xc_copied qkv_mm qk_ready v_ready scores_mm smax_done sub_done exp_done
            p_tr p_copied pv_mm rden_done o_norm o_tr o_copied wo_mm bo_added x_attn
            m_ln m_mean m_ready m_xn_ready ew1_split
            mx_tr mx_copied mx_hi_done mx_lo_done hid_mm gate_mm relu_v relu_a gate_v exp_gate gate_done
            eb_mult eb_v eb_added y_mm y_v
            x_max h_max sc_v sc_ready sc_late sc_set q1_done xq_ready xq_tr xhi_copied xlo_done xlo_copied
            conv_mm hpre_done silu_done q2_ready
            q2_tr q2_copied out_mm x_out""".split()
        s = {n: sem(n) for n in names}
        x_in = [sem(f"x_in{i}") for i in range(2)]
        ctx_ld = [sem(f"ctx_ld{i}") for i in range(2)]
        stored = sem("stored")

        def wait(eng, name, value):
            if isinstance(value, int) and value <= 0:
                return
            eng.wait_ge(s[name], value)

        def lead_in(step, first, last, T=T):
            for t in range(first, last + 1):
                step(t, t % 2, lambda k: 0 <= t + k < T)

        def run_tiles(eng, step, lead, lag, lo=2, T=T, first=None, before=(), body=2):
            before = dict(before)
            n = (T - lead - lo) // body

            def straight(first, end):
                for t in range(first, end):
                    if t in before:
                        before[t]()
                    step(t, t % 2, lambda k: 0 <= t + k < T)

            straight(-lead if first is None else first, lo)
            if lo in before:
                before[lo]()
            with eng.Fori(0, n) as i:
                for k in range(body):
                    step(i * body + (lo + k), k % 2, lambda k: True)
            straight(lo + body * n, T + lag)

        LN0 = {0: 0, 2: T, 3: 2 * T}

        def x_tile(t):
            return x_all[:, bass.ds(t * D, D)]

        def ln_stats(dve, f, t, par):
            n = LN0[f] + t
            if f == 0:
                dve.wait_ge(x_in[par], (t + (2 - par)) * 8)
            else:
                wait(dve, {2: "y_v", 3: "x_attn"}[f], {2: E * (t + 1), 3: T + t + 1}[f])
            wait(dve, "ln_mv", n - 1)
            dve.bn_stats(ln_st[:, par, :], x_tile(t)).then_inc(s["ln"], 1)

        def ln_mean_ready(dve, f, t):
            n = LN0[f] + t
            wait(dve, "ln_ready", LN_STEPS * (n - 1))
            wait(dve, "ln", n + 1)

        def ln_mean(dve, par):
            dve.bn_aggr(ln_mv[:, par, :], ln_st[:, par, :]).then_inc(s["ln_mv"], 1)

        LN_STEPS = 4

        def ln_rstd(pool, f, t, par):
            n = LN0[f] + t
            m = LN_STEPS * n

            def step(out, a, b, op):
                pool.tensor_tensor(out, a, b, op).then_inc(s["ln_ready"], 1)

            wait(pool, "ln_mv", n + 1)
            wait(pool, "xn_ready", n - 1)
            step(ln_ve[:, par, :], ln_mv[:, par, 1:2], const[:, C_EPS:C_EPS + 1], ALU.add)
            step(ln_nm[:, par, :], ln_mv[:, par, 0:1], const[:, C_NEG:C_NEG + 1], ALU.mult)
            pool.wait_ge(s["ln_ready"], m + 2)
            step(ln_rs[:, par, :], ln_ve[:, par, :], const[:, C_POW:C_POW + 1], ALU.pow)
            pool.wait_ge(s["ln_ready"], m + 3)
            step(ln_nr[:, par, :], ln_nm[:, par, :], ln_rs[:, par, :], ALU.mult)

        def ln_apply(act, f, t, par, free, free_at):
            n = LN0[f] + t
            wait(act, "ln_ready", LN_STEPS * (n + 1))
            wait(act, free, free_at)
            act.activation(xn[:, par, :], x_tile(t), ACT.Identity, bias=ln_nr[:, par, :],
                           scale=ln_rs[:, par, :]).then_inc(s["xn_ready"], 1)

        MOE_LOADS = 10
        TERN_DVE = 4
        GATE_STEPS = 16

        block = ctx.enter_context(nc.Block())

        @block.sync
        def _(sp):
            def load(dst, src, name):
                sp.dma_start(dst, src).then_inc(s[name], 16)

            def col(v):
                return v.rearrange("(p o) -> p o", o=1)

            def attention_weights(L):
                for n, w in enumerate("qkvo"):
                    load(w_raw[:, L, n, :], a[f"L{L}_xattn_W{w}"], "attn_w_in")
                for n, w in enumerate("qkv"):
                    load(b_col[:, L, n:n + 1], col(a[f"L{L}_xattn_b{w}"]), "attn_w_in")
                load(bo_row[:, L, :], a[f"L{L}_xattn_bo"].partition_broadcast(P), "attn_w_in")

            load(const[:], a["const"], "const_in")
            load(graw[:, 0:2], a["g_xattn"].partition_broadcast(P), "g_in")
            load(graw[:, 2:4], a["g_ffn"].partition_broadcast(P), "g_in")

            x_d = a["x"].rearrange("b s d -> (b s) d")
            c_d = a["ctx_1024"].rearrange("b s d -> (b s) d")
            o_d = out.rearrange("b s d -> (b s) d")

            def load_ctx(L, t, par):
                wait(sp, "xc_tr", L * T + t - 1)
                sp.dma_start(ctx_in[:, par, :], c_d[bass.ds(t * P, P), :]).then_inc(ctx_ld[par], 16)

            def attention0(t, par, has):
                if has(3):
                    if not isinstance(t, int) or t + 3 >= 2:
                        wait(sp, "ln", t + 2)
                    sp.dma_start(x_all[:, bass.ds((t + 3) * D, D)], x_d[bass.ds((t + 3) * P, P), :])\
                        .then_inc(x_in[1 - par], 16)
                if has(1):
                    load_ctx(0, t + 1, 1 - par)

            def later_weights():
                attention_weights(1)
                for b in range(BT):
                    load(m_int[b * S:(b + 1) * S, :], a["mask_1x1xSxS2_ik0"][0, 0], "mask_in")
                load(gate_w[:, 0:E], a["L0_ffn_gate_w"], "moe_w_in")
                load(gate_w[:, E:GW], a["L0_ffn_dp_w1"], "moe_w_in")
                load(gate_b[:, 0:E], a["L0_ffn_gate_b"].partition_broadcast(P), "moe_w_in")
                load(gate_b[:, E:GW], a["L0_ffn_dp_b1"].partition_broadcast(P), "moe_w_in")
                load(dp_w2[:], a["L0_ffn_dp_w2"].rearrange("h o -> (h o)").partition_broadcast(P), "moe_w_in")
                load(dp_b2[:], a["L0_ffn_dp_b2"].partition_broadcast(P), "moe_w_in")
                load(ew1[:], a["L0_ffn_ew1"].rearrange("e d h -> d e h"), "moe_w_in")
                load(ew2[:], a["L0_ffn_ew2"].rearrange("e (c h) d -> h (e c) d", c=2), "moe_w_in")
                sp.dma_start(eb1[:], a["L0_ffn_eb1"].rearrange("e (c h) -> h (e c)", c=2),
                             allow_slow_non_contiguous=True).then_inc(s["moe_w_in"], 16)
                load(eb2[:], a["L0_ffn_eb2"].rearrange("e d -> (e d)").partition_broadcast(P), "moe_w_in")
                load(f_w1[:], a["L1_ffn_w1"].rearrange("(c p) d -> p c d", p=P), "ffn_w_in")
                load(f_w2[:], a["L1_ffn_w2"], "ffn_w_in")
                load(f_cw[:], a["L1_ffn_conv_w"].rearrange("(c p) o k -> p c (o k)", p=P), "ffn_w_in")
                load(f_cb[:], a["L1_ffn_conv_b"].partition_broadcast(P), "ffn_w_in")

            lead_in(attention0, -3, -2)
            attention_weights(0)
            run_tiles(sp, attention0, 3, 0, first=-1, before={2: later_weights})

            def attention1(t, par, has):
                if has(1):
                    load_ctx(1, t + 1, 1 - par)

            run_tiles(sp, attention1, 1, 0)

            def store(t, par, has):
                wait(sp, "x_out", t + 1)
                sp.dma_start(o_d[bass.ds(t * P, P), :], x_tile(t)).then_inc(stored, 16)

            run_tiles(sp, store, 0, 0)
            sp.wait_ge(stored, 16 * T)

        @block.gpsimd
        def _(pool):
            pool.memset(x_lo[:], 0.0).then_inc(s["zero_set"], 1)
            pool.wait_ge(s["const_in"], 16)

            def attention(L):
                def step(t, par, has):
                    if has(3):
                        ln_rstd(pool, 2 * L, t + 3, 1 - par)
                    if has(1):
                        n = L * T + t + 1
                        wait(pool, "xn_ready", L * T + t + 2)
                        pool.tensor_tensor(x_tile(t + 1), x_tile(t + 1), bo_row[:, L, :], ALU.add)\
                            .then_inc(s["bo_added"], 1)
                return step

            pool.wait_ge(s["setup_v"], 1)

            def experts(u, par, has):
                def add_biases(k, j):
                    t = G * (u + k) + j
                    wait(pool, "eb_mult", E * (t + 1))
                    wait(pool, "eb_added", t)
                    pool.tensor_tensor(eb_acc[:, :, :], eb_t[:, j % 2, 0:2, :], eb_t[:, j % 2, 2:4, :], ALU.add)\
                        .then_inc(s["eb_v"], 1)
                    pool.wait_ge(s["eb_v"], 2 * t + 1)
                    pool.tensor_tensor(eb_sum[:], eb_acc[:, 0, :], eb_acc[:, 1, :], ALU.add)\
                        .then_inc(s["eb_v"], 1)
                    pool.wait_ge(s["eb_v"], 2 * t + 2)
                    pool.tensor_tensor(x_tile(t), x_tile(t), eb_sum[:], ALU.add).then_inc(s["eb_added"], 1)

                if has(0):
                    add_biases(0, 2)
                    add_biases(0, 3)
                if has(1):
                    add_biases(1, 0)
                    add_biases(1, 1)
                if has(3):
                    m = 4 * (u + 3)

                    def step(out, a, b, op):
                        pool.tensor_tensor(out, a, b, op).then_inc(s["m_ready"], 1)

                    def all_tiles(c):
                        return const[:, c:c + 1].to_broadcast([P, G])

                    wait(pool, "m_mean", G * (u + 4))
                    wait(pool, "m_xn_ready", G * (u + 2))
                    step(m_ve[:, 1 - par, :], m_mv[:, 1 - par, :, 1], all_tiles(C_EPS), ALU.add)
                    step(m_nm[:, 1 - par, :], m_mv[:, 1 - par, :, 0], all_tiles(C_NEG), ALU.mult)
                    pool.wait_ge(s["m_ready"], m + 2)
                    step(m_rs[:, 1 - par, :], m_ve[:, 1 - par, :], all_tiles(C_POW), ALU.pow)
                    pool.wait_ge(s["m_ready"], m + 3)
                    step(m_nr[:, 1 - par, :], m_nm[:, 1 - par, :], m_rs[:, 1 - par, :], ALU.mult)

            attention1 = attention(1)
            w1_flat = f_w1[:].rearrange("p c d -> p (c d)")

            def ternary(w, i):
                k = TERN_DVE + 3 * i
                pool.wait_ge(s["tern"], k)
                pool.tensor_scalar(w, w, f_s[:, 4 + i:5 + i], ROUND, ALU.mult, ALU.add).then_inc(s["tern"], 1)
                pool.wait_ge(s["tern"], k + 1)
                pool.tensor_scalar(w, w, -ROUND, 1.0, ALU.add, ALU.min).then_inc(s["tern"], 1)
                pool.wait_ge(s["tern"], k + 2)
                pool.tensor_scalar(w, w, -1.0, 0.0, ALU.max, ALU.add).then_inc(s["tern"], 1)

            def tap_weights(tap):
                pool.wait_ge(s["tern"], TERN_DVE + 3)
                for c in range(FC):
                    pool.tensor_scalar(f_tap[:, tap, c, :], f_w1[:, c, :], f_cw[:, c, tap:tap + 1], 0.0,
                                       ALU.mult, ALU.add).then_inc(s["tap_ready"], 1)

            run_tiles(pool, attention(0), 3, 0, body=4, before={T - 2: lambda: lead_in(experts, -3, -2, NG)})
            run_tiles(pool, experts, 3, 0, T=NG, first=-1, before={
                NG - 3: lambda: ternary(w1_flat, 0),
                NG - 2: lambda: (lead_in(attention1, -3, -2), ternary(f_w2[:], 1)),
                NG - 1: lambda: (pool.wait_ge(s["setup_v"], 3), lead_in(attention1, -1, -1), tap_weights(0))})
            run_tiles(pool, attention1, 3, 0, first=0, body=4, before={
                0: lambda: tap_weights(1), 1: lambda: tap_weights(2)})

            def ffn(t, par, has):
                o = 1 - par
                if has(4):
                    ln_rstd(pool, 3, t + 4, par)
                if has(2):
                    wait(pool, "q1_done", t + 3)
                else:
                    if has(-2):
                        wait(pool, "sc_ready", t + 3)
                        wait(pool, "q2_tr", t - 3)
                    if has(1):
                        wait(pool, "xhi_copied", t + 2)
                        wait(pool, "xlo_copied", t + 1)
                if has(1):
                    pool.tensor_tensor(x_lo[:], x_t[:, o, :], tap_hi[:, o, 1, :, :].rearrange("p b s -> p (b s)"),
                                       ALU.subtract).then_inc(s["xlo_done"], 1)
                if has(2):
                    pool.tensor_scalar(xdq[:, par, :], q1[:], -ROUND, sc_i[:, o, 0:1], ALU.add, ALU.mult)\
                        .then_inc(s["xq_ready"], 1)
                if has(-2):
                    pool.tensor_scalar(q2[:, par, :], hact[:, par, :], sc_q[:, o, 1:2], ROUND, ALU.mult, ALU.add)\
                        .then_inc(s["q2_ready"], 1)

            run_tiles(pool, ffn, 4, 2, lo=4, body=4)

        @block.scalar
        def _(act):
            act.wait_ge(s["g_in"], 32)
            act.activation(tg[:], graw[:], ACT.Tanh).then_inc(s["tanh_done"], 1)
            act.wait_ge(s["tanh_done"], 1)
            def copy_weights(L):
                act.wait_ge(s["w_tr"], L + 1)
                act.activation(w_t[:, L, 0:3, :], bank[5 * L][:, 0:3 * P], ACT.Copy).then_inc(s["w_copied"], 1)
                act.activation(w_t[:, L, 3, :], bank[5 * L][:, 3 * P:], ACT.Copy, scale=tg[:, L:L + 1])\
                    .then_inc(s["w_copied"], 1)

            copy_weights(0)

            def attention(L):
                def step(t, par, has):
                    n = L * T + t
                    o = 1 - par
                    if has(1):
                        wait(act, "xc_tr", n + 2)
                        wait(act, "qkv_mm", n)
                        act.activation(xct[:, o, :, :, :, :].rearrange("p a b c k -> p (a b) c k"),
                                       bank[4][:, 0:2 * P].rearrange("p (a k) -> p a k", k=S).unsqueeze(2)
                                       .to_broadcast([P, 2 * BT, 2, S]), ACT.Copy).then_inc(s["xc_copied"], 1)
                    if has(-2):
                        wait(act, "o_tr", n - 1)
                        wait(act, "wo_mm", n - 2)
                        act.activation(o_t[:], bank[7][:, 0:P], ACT.Identity, bias=b_col[:, L, 2:3])\
                            .then_inc(s["o_copied"], 1)
                    if has(-1):
                        for half in range(2):
                            wait(act, "p_tr", 2 * (n - 1) + half + 1)
                            wait(act, "pv_mm", n - 1)
                            act.activation(prob_t[:, 4 * half:4 * half + 4, :], bank[2 + half][:], ACT.Copy)\
                                .then_inc(s["p_copied"], 1)
                    if has(0):
                        for half in range(2):
                            wait(act, "sub_done", 2 * n + half + 1)
                            v = prob[:, par, half * 512:(half + 1) * 512]
                            act.activation(v, v, ACT.Exp, scale=SCALE).then_inc(s["exp_done"], 1)
                    if has(2):
                        ln_apply(act, 2 * L, t + 2, par, "xc_tr", n + 1)
                return step

            def bias_products(u, par, k, j):
                t = G * (u + k) + j
                wait(act, "eb_v", 2 * (t - 2) + 1)
                for e in range(E):
                    act.activation(eb_t[:, j % 2, e, :], eb2[:, e * P:(e + 1) * P], ACT.Copy,
                                   scale=gwt[:, 1 - par if k else par, j, e:e + 1]).then_inc(s["eb_mult"], 1)

            def experts_hidden(u, par, has):
                o = 1 - par

                def relu(c):
                    wait(act, "hid_mm", EC * u + c + 1)
                    if c == 0:
                        wait(act, "y_mm", G * u)
                    act.activation(hid[:, c, :], bank[c % 4][:], ACT.Relu, bias=eb1[:, c:c + 1])\
                        .then_inc(s["relu_a"], 1)

                if has(0):
                    relu(0)
                    relu(2)
                if has(1):
                    wait(act, "mx_tr", u + 2)
                    wait(act, "gate_mm", u + 1)
                    act.activation(mxt[:], bank[4][:], ACT.Copy).then_inc(s["mx_copied"], 1)
                    wait(act, "hid_mm", EC * u)
                    act.activation(mx_hi[:, o, :], bank[4][:], ACT.Copy).then_inc(s["mx_hi_done"], 1)
                if has(0):
                    relu(4)
                    relu(6)
            def experts_gate(u, par, has):
                if has(0):
                    bias_products(u, par, 0, 2)
                    bias_products(u, par, 0, 3)
                if has(1):
                    wait(act, "gate_v", GATE_STEPS * (u + 1) + 6)
                    act.activation(ge[:], gls[:], ACT.Exp).then_inc(s["exp_gate"], 1)
                if has(2):
                    wait(act, "m_ready", 4 * (u + 3))
                    wait(act, "mx_tr", u + 2)
                    for j in range(G):
                        act.activation(m_xn[:, j, :], x_tile(G * (u + 2) + j), ACT.Identity,
                                       bias=m_nr[:, par, j:j + 1], scale=m_rs[:, par, j:j + 1])\
                            .then_inc(s["m_xn_ready"], 1)
                if has(1):
                    wait(act, "gate_done", u + 2)
                    bias_products(u, par, 1, 0)
                    bias_products(u, par, 1, 1)

            def experts(u, par, has):
                experts_hidden(u, par, has)
                experts_gate(u, par, has)

            def experts_start():
                act.wait_ge(s["moe_w_in"], 16 * MOE_LOADS)
                act.activation(ew1_hi[:].rearrange("p c h -> p (c h)"), ew1[:].rearrange("p e h -> p (e h)"), ACT.Copy)\
                    .then_inc(s["ew1_split"], 1)
                lead_in(experts, -2, -2, NG)

            attention1 = attention(1)
            run_tiles(act, attention(0), 3, 2, body=4, before={
                T - 1: experts_start,
                T: lambda: (copy_weights(1), lead_in(experts_hidden, -1, -1, NG)),
                T + 1: lambda: lead_in(experts_gate, -1, -1, NG)})
            run_tiles(act, experts, 2, 0, T=NG, first=0, before={
                NG - 2: lambda: lead_in(attention1, -3, -2), NG - 1: lambda: lead_in(attention1, -1, -1)})

            def ffn(t, par, has):
                o = 1 - par
                if has(-1):
                    wait(act, "hpre_done", t)
                    wait(act, "q2_ready", t - 2)
                    act.activation(hact[:, o, :], hpre[:, o, :], ACT.Silu).then_inc(s["silu_done"], 1)
                if has(2):
                    wait(act, "sc_ready", t + 3)
                    wait(act, "xq_ready", t + 2)
                    act.activation(q1[:], xn[:, par, :], ACT.Identity, scale=sc_q[:, o, 0:1],
                                   bias=const[:, C_RND:C_RND + 1]).then_inc(s["q1_done"], 1)
                if has(4):
                    ln_apply(act, 3, t + 4, par, "q1_done", t + 3)
                if has(1):
                    wait(act, "xlo_done", t + 2)
                    if not has(2):
                        wait(act, "conv_mm", t)
                    shifted(tap_lo[:, o], x_lo[:], "xlo_copied")
                if has(2):
                    wait(act, "xq_tr", t + 3)
                    act.activation(x_t[:, par, :], bank[4][:, 0:P], ACT.Copy)
                    shifted(tap_hi[:, par], bank[4][:, 0:P], "xhi_copied")

            def shifted(dst, src, name):
                src = src.rearrange("p (b s) -> p b s", b=BT)
                act.activation(dst[:, 0, :, 1:S], src[:, :, 0:S - 1], ACT.Copy)
                act.activation(dst[:, 1, :, :], src, ACT.Copy)
                act.activation(dst[:, 2, :, 0:S - 1], src[:, :, 1:S], ACT.Copy).then_inc(s[name], 1)

            def ffn_start():
                act.wait_ge(s["xc_tr"], 2 * T)
                act.wait_ge(s["zero_set"], 1)
                for tap in (tap_hi, tap_lo):
                    for par in range(2):
                        act.activation(tap[:, par, 0, :, 0], x_lo[:, 0:BT], ACT.Copy)
                        act.activation(tap[:, par, 2, :, S - 1], x_lo[:, 0:BT], ACT.Copy).then_inc(s["edges_set"], 1)
                lead_in(ffn, -5, -3)

            def copy_ffn_weights():
                for k in range(TAPS):
                    act.wait_ge(s["tap_tr"], k + 1)
                    act.activation(f_wk_hi[:, k, :], bank[k][:], ACT.Copy).then_inc(s["tap_copied"], 1)
                act.wait_ge(s["tap_tr"], TAPS + 1)
                act.activation(f_w2t[:].rearrange("p c d -> p (c d)"), bank[3][:], ACT.Copy)\
                    .then_inc(s["w2t_copied"], 1)
                lead_in(ffn, -1, -1)

            run_tiles(act, attention1, 3, 2, first=0, body=4, before={
                T - 1: ffn_start, T: lambda: lead_in(ffn, -2, -2), T + 1: copy_ffn_weights})
            run_tiles(act, ffn, 5, 1, lo=4, first=0, body=4)

        @block.vector
        def _(dve):
            dve.wait_ge(s["const_in"], 16)
            dve.tensor_copy(ident16[:], ident).then_inc(s["ident16_done"], 1)
            for par in range(2):
                for b in range(BT):
                    dve.tensor_copy(vb[:, par, :, b, :, HD:VW],
                                    const[:, C_H:C_H + 2].unsqueeze(1).unsqueeze(3).to_broadcast([P, NPAIR, 2, 1]))\
                        .then_inc(s["ones_set"], 1)
            dve.wait_ge(s["attn_w_in"], 16 * 8)
            dve.wait_ge(s["tanh_done"], 1)

            def scale_bo(L):
                dve.tensor_scalar(bo_row[:, L, :], bo_row[:, L, :], tg[:, L:L + 1], None, ALU.mult)\
                    .then_inc(s["setup_v"], 1)

            scale_bo(0)
            dve.tensor_copy(q_mask[:, 0, :, :], const[:, C_R:C_R + RQ].unsqueeze(2).to_broadcast([P, RQ, P]))\
                .then_inc(s["setup_v"], 1)
            dve.wait_ge(s["setup_v"], 2)

            def masks():
                dve.wait_ge(s["attn_w_in"], 16 * 16)
                scale_bo(1)
                dve.wait_ge(s["mask_in"], 32)
                dve.tensor_scalar(m_keep[:], m_int[:], 0.0, None, ALU.not_equal).then_inc(s["mask_v"], 1)
                dve.wait_ge(s["mask_v"], 1)
                dve.tensor_reduce(m_any[:], m_keep[:], AX.X, ALU.max).then_inc(s["mask_v"], 1)
                dve.wait_ge(s["mask_v"], 2)
                dve.tensor_scalar(m_dead[:], m_any[:], -1.0, 1.0, ALU.mult, ALU.add).then_inc(s["mask_v"], 1)
                dve.tensor_scalar(m_diag[:], const[0:S, C_ID:C_ID + S], m_any[0:S, :], None, ALU.mult)\
                    .then_inc(s["mask_v"], 1)
                dve.wait_ge(s["mask_v"], 4)
                dve.tensor_scalar(m_keep2[:], m_keep[:], m_dead[:], 1.0, ALU.max, ALU.subtract).then_inc(s["mask_v"], 1)
                dve.wait_ge(s["mask_v"], 5)
                dve.tensor_scalar(neg_mask[:], m_keep2[:], NEG, None, ALU.mult).then_inc(s["mask_v"], 1)

            def query_masks():
                dve.wait_ge(s["alive_mm"], 1)
                for r in range(RQ):
                    dve.tensor_scalar(q_mask[:, 1, r, :].rearrange("p (b s) -> p b s", b=BT),
                                      bank[4][:, 0:S].unsqueeze(1).to_broadcast([P, BT, S]),
                                      const[:, C_R + r:C_R + r + 1], None, ALU.mult).then_inc(s["setup_v"], 1)

            def attention(L):
                def step(t, par, has):
                    n = L * T + t
                    o = 1 - par
                    if has(-2):
                        wait(dve, "pv_mm", n - 1)
                        wait(dve, "o_tr", n - 3)
                        ov = bank[6][:, 0:NPAIR * BT * 2 * VW].rearrange("p (i b h v) -> p i b h v", i=NPAIR, b=BT, h=2)
                        rv = rden[:].rearrange("p (i h) -> p i h", h=2)
                        onv = o_n[:, par, :].rearrange("p (i h v) -> p i h v", i=NPAIR, h=2)
                        wait(dve, "o_norm", 2 * (n - 2))
                        for b in range(BT):
                            q = slice(b * S, (b + 1) * S)
                            dve.reciprocal(rv[q], ov[q, :, b, :, HD]).then_inc(s["rden_done"], 1)
                    if has(0):
                        wait(dve, "pv_mm", n - 1)
                        wait(dve, "qkv_mm", n + 1)
                        for b in range(BT):
                            dve.tensor_tensor(
                                vb[:, par, :, b, :, 0:HD],
                                bank[5][:, (2 + b) * P:(3 + b) * P].rearrange("p (i h v) -> p i h v", i=NPAIR, h=2),
                                const[:, C_H:C_H + 2].unsqueeze(1).unsqueeze(3).to_broadcast([P, NPAIR, 2, HD]),
                                ALU.mult).then_inc(s["v_ready"], 1)
                    if has(-2):
                        dve.wait_ge(s["rden_done"], 2 * (n - 1))
                        for b in range(BT):
                            q = slice(b * S, (b + 1) * S)
                            dve.tensor_tensor(onv[q], ov[q, :, b, :, 0:HD],
                                              rv[q].unsqueeze(3).to_broadcast([S, NPAIR, 2, HD]), ALU.mult)\
                                .then_inc(s["o_norm"], 1)
                    if has(0):
                        for half in range(2):
                            wait(dve, "scores_mm", 2 * n + half + 1)
                            sc = bank[half][:].rearrange("p (h k) -> p h k", k=S)
                            m = smax[:, half * 8:half * 8 + 8]
                            wait(dve, "sub_done", 2 * n + half - 1)
                            dve.tensor_reduce(m, sc, AX.X, ALU.max).then_inc(s["smax_done"], 1)
                            dve.wait_ge(s["smax_done"], 2 * n + half + 1)
                            wait(dve, "p_tr", 2 * (n - 1))
                            dve.tensor_tensor(prob[:, par, half * 512:(half + 1) * 512].rearrange("p (h k) -> p h k", k=S),
                                              sc, m.unsqueeze(2).to_broadcast([P, 8, S]), ALU.subtract)\
                                .then_inc(s["sub_done"], 1)
                    if has(3):
                        ln_stats(dve, 2 * L, t + 3, o)
                        ln_mean_ready(dve, 2 * L, t + 3)
                    if has(1):
                        wait(dve, "qkv_mm", n + 2)
                        wait(dve, "scores_mm", 2 * n)
                        dve.scalar_tensor_tensor(
                            out=qq[:, o, :, :], in0=bank[5][:, 0:P].unsqueeze(1).to_broadcast([P, RQ, P]),
                            scalar=b_col[:, L, 0:1], in1=q_mask[:, L, :, :], op0=ALU.add, op1=ALU.mult)\
                            .then_inc(s["qk_ready"], 1)
                        dve.scalar_tensor_tensor(
                            out=kj[:, o, :, :], in0=bank[5][:, P:2 * P].unsqueeze(1).to_broadcast([P, JH, P]),
                            scalar=b_col[:, L, 1:2],
                            in1=const[:, C_J:C_J + JH].unsqueeze(2).to_broadcast([P, JH, P]),
                            op0=ALU.add, op1=ALU.mult).then_inc(s["qk_ready"], 1)
                    if has(3):
                        ln_mean(dve, o)
                    if has(-2):
                        wait(dve, "wo_mm", n - 1)
                        wait(dve, "bo_added", n - 1)
                        dve.tensor_tensor(x_tile(t - 2), bank[7][:, P:2 * P], x_tile(t - 2), ALU.add)\
                            .then_inc(s["x_attn"], 1)
                return step

            def experts(u, par, has):
                o = 1 - par
                m0 = GATE_STEPS * (u + 1)
                lg = gl[:, :, 0:E]

                def gate(ins):
                    ins.then_inc(s["gate_v"], 1)

                def after(k):
                    dve.wait_ge(s["gate_v"], m0 + k)

                def relu(c):
                    wait(dve, "hid_mm", EC * u + c + 1)
                    if c == 1:
                        wait(dve, "y_mm", G * u)
                    dve.tensor_scalar(hid[:, c, :], bank[c % 4][:], eb1[:, c:c + 1], 0.0, ALU.add, ALU.max)\
                        .then_inc(s["relu_v"], 1)

                def combine(j, e):
                    t = G * u + j
                    src = x_tile(t) if e == 0 else y_acc[:, (e - 1) % 2, :]
                    dst = x_tile(t) if e == E - 1 else y_acc[:, e % 2, :]
                    if e == 0:
                        wait(dve, "y_mm", t + 1)
                        wait(dve, "eb_added", t + 1)
                    wait(dve, "y_v", E * t + e)
                    dve.scalar_tensor_tensor(out=dst, in0=bank[6 + j % 2][:, e * P:(e + 1) * P],
                                             scalar=gwt[:, par, j, e:e + 1], in1=src, op0=ALU.mult, op1=ALU.add)\
                        .then_inc(s["y_v"], 1)

                def per_tile(v, n):
                    return v[:].unsqueeze(2).to_broadcast([P, G, n])

                if has(0):
                    relu(1)
                    relu(3)
                if has(1):
                    wait(dve, "mx_hi_done", u + 2)
                    wait(dve, "hid_mm", EC * u)
                    dve.tensor_tensor(mx_lo[:, o, :], bank[4][:], mx_hi[:, o, :], ALU.subtract)\
                        .then_inc(s["mx_lo_done"], 1)
                if has(0):
                    relu(5)
                if has(0):
                    relu(7)
                if has(1):
                    wait(dve, "gate_mm", u + 2)
                    wait(dve, "gate_done", u + 1)
                    gate(dve.tensor_tensor(gl[:], bank[5][:, 0:G * GW].rearrange("p (g w) -> p g w", g=G),
                                              gate_b[:].unsqueeze(1).to_broadcast([P, G, GW]), ALU.add))
                    after(1)
                    gate(dve.scalar_tensor_tensor(out=gj[:], in0=gl[:, :, E:GW], scalar=0.0,
                                                     in1=dp_w2[:].unsqueeze(1).to_broadcast([P, G, DPH]),
                                                     op0=ALU.max, op1=ALU.mult))
                    gate(dve.tensor_reduce(gm[:], lg, AX.X, ALU.max))
                    l_row = lg.unsqueeze(2).to_broadcast([P, G, E, E])
                    l_col = lg.unsqueeze(3).to_broadcast([P, G, E, E])
                    tie = const[:, C_TIE:C_TIE + E * E].unsqueeze(1).to_broadcast([P, G, E * E])
                    gate(dve.tensor_tensor(g_gt[:], l_row, l_col, ALU.is_gt))
                    gate(dve.tensor_tensor(g_eq[:], l_row, l_col, ALU.is_equal))
                    after(3)
                    wait(dve, "exp_gate", u + 1)
                    gate(dve.tensor_tensor(gls[:], lg, per_tile(gm, E), ALU.subtract))
                    after(5)
                    eq = g_eq[:].rearrange("p g e f -> p g (e f)")
                    gate(dve.tensor_tensor(eq, eq, tie, ALU.mult))
                    gate(dve.tensor_reduce(gz[:], gj[:], AX.X, ALU.add))
                    after(7)
                    gate(dve.tensor_tensor(g_gt[:], g_gt[:], g_eq[:], ALU.add))
                    after(8)
                    gate(dve.tensor_tensor(gs3[:], thr[:].unsqueeze(1).to_broadcast([P, G, E - 1]),
                                               per_tile(gz, E - 1), ALU.is_le))
                if has(0):
                    combine(0, 0)
                if has(1):
                    after(9)
                    gate(dve.tensor_reduce(g_rank[:], g_gt[:], AX.X, ALU.add))
                    after(10)
                    gate(dve.tensor_reduce(gk[:], gs3[:], AX.X, ALU.add))
                if has(0):
                    combine(0, 1)
                if has(1):
                    after(12)
                    gate(dve.tensor_tensor(g_sel[:], g_rank[:], per_tile(gk, E), ALU.is_le))
                if has(0):
                    combine(0, 2)
                if has(1):
                    after(13)
                    wait(dve, "exp_gate", u + 2)
                    gate(dve.tensor_tensor(g_ew[:], g_sel[:], ge[:], ALU.mult))
                if has(0):
                    combine(0, 3)
                if has(1):
                    after(14)
                    gate(dve.tensor_reduce(g_sum[:], g_ew[:], AX.X, ALU.add))
                if has(0):
                    combine(1, 0)
                if has(1):
                    after(15)
                    gate(dve.reciprocal(g_rs[:], g_sum[:]))
                if has(0):
                    combine(1, 1)
                if has(1):
                    after(16)
                    wait(dve, "y_v", E * G * u)
                    wait(dve, "eb_mult", E * G * u)
                    dve.scalar_tensor_tensor(out=gwt[:, o, :, :], in0=g_ew[:], scalar=tg[:, 2:3],
                                             in1=per_tile(g_rs, E), op0=ALU.mult, op1=ALU.mult)\
                        .then_inc(s["gate_done"], 1)
                if has(0):
                    combine(1, 2)
                    combine(1, 3)
                if has(3):
                    for j in range(G):
                        wait(dve, "x_attn", G * (u + 3) + j + 1)
                        if j == 0:
                            wait(dve, "m_mean", G * (u + 2))
                        dve.bn_stats(m_st[:, o, j, :], x_tile(G * (u + 3) + j)).then_inc(s["m_ln"], 1)
                if has(0):
                    for e in range(E):
                        combine(2, e)
                if has(3):
                    wait(dve, "m_ready", 4 * (u + 2))
                    wait(dve, "m_ln", G * (u + 4))
                if has(0):
                    combine(3, 0)
                if has(3):
                    for j in range(G):
                        dve.bn_aggr(m_mv[:, o, j, :], m_st[:, o, j, :]).then_inc(s["m_mean"], 1)
                if has(0):
                    for e in range(1, E):
                        combine(3, e)

            def experts_start():
                masks()
                dve.wait_ge(s["moe_w_in"], 16 * MOE_LOADS)
                dve.tensor_scalar(thr[:], const[:, C_THR:C_THR + E - 1], dp_b2[:], None, ALU.subtract)\
                    .then_inc(s["thr_done"], 1)
                lead_in(experts, -3, -2, NG)

            def tern(ins):
                ins.then_inc(s["tern"], 1)

            def weight_sums():
                dve.wait_ge(s["ffn_w_in"], 64)
                dve.tensor_reduce(f_s[:, 0:1], f_w1[:].rearrange("p c d -> p (c d)"), AX.X, ALU.add,
                                  apply_absolute_value=True).then_inc(s["ffn_sum"], 1)
                dve.tensor_reduce(f_s[:, 1:2], f_w2[:], AX.X, ALU.add, apply_absolute_value=True)\
                    .then_inc(s["ffn_sum"], 1)

            def weight_scales():
                query_masks()
                dve.wait_ge(s["sum_mm"], 1)
                tern(dve.tensor_scalar(f_s[:, 2:4], bank[4][:, S:S + 2], 1.0 / (F * D), Q_EPS, ALU.mult, ALU.max))
                dve.wait_ge(s["ew1_split"], 1)
                dve.tensor_tensor(ew1_lo[:].rearrange("p c h -> p (c h)"), ew1[:].rearrange("p e h -> p (e h)"),
                                  ew1_hi[:].rearrange("p c h -> p (c h)"), ALU.subtract).then_inc(s["ew1_split"], 1)

            def experts_lead():
                dve.wait_ge(s["thr_done"], 1)
                lead_in(experts, -1, -1, NG)

            def ffn_scales():
                dve.wait_ge(s["tern"], 1)
                tern(dve.reciprocal(f_s[:, 4:6], f_s[:, 2:4]))
                tern(dve.tensor_scalar(f_cw[:], f_cw[:], f_s[:, 2:3], None, ALU.mult))
                tern(dve.tensor_scalar(f_s[:, 6:7], f_s[:, 3:4], tg[:, 3:4], 1.0 / 127.0, ALU.mult, ALU.mult))
                dve.wait_ge(s["tern"], TERN_DVE)
                dve.tensor_scalar(sc_f[:, 0:1], ones[:, 0:1], 1.0 / 127.0, None, ALU.mult).then_inc(s["sc_set"], 1)
                dve.tensor_scalar(sc_f[:, 1:2], f_s[:, 6:7], 1.0, None, ALU.mult).then_inc(s["sc_set"], 1)
                dve.tensor_scalar(sc_m[:], ones[:, 0:2], 1.0, None, ALU.mult).then_inc(s["sc_set"], 1)

            attention1 = attention(1)
            run_tiles(dve, attention(0), 3, 2, lo=4, body=4, before={
                T - 3: experts_start, T - 2: weight_sums, T - 1: weight_scales, T + 1: experts_lead})
            run_tiles(dve, experts, 3, 0, T=NG, first=0, before={
                NG - 4: ffn_scales,
                NG - 2: lambda: lead_in(attention1, -3, -2),
                NG - 1: lambda: (dve.wait_ge(s["setup_v"], 7), lead_in(attention1, -1, -1))})

            def ffn(t, par, has):
                o = 1 - par
                scales = has(3) or has(-1)
                if has(-3):
                    wait(dve, "q2_tr", t - 2)
                    dve.tensor_scalar(q2t[:, o, :], bank[5][:], ROUND, 127.0, ALU.subtract, ALU.min)\
                        .then_inc(s["q2_copied"], 1)
                if has(-4):
                    if not has(-3):
                        wait(dve, "out_mm", t - 3)
                    if not has(-2):
                        wait(dve, "sc_late", t - 3)
                    dve.scalar_tensor_tensor(out=x_tile(t - 4), in0=bank[6][:, 0:P], scalar=sc_l[:],
                                             in1=x_tile(t - 4), op0=ALU.mult, op1=ALU.add).then_inc(s["x_out"], 1)
                if has(5):
                    ln_stats(dve, 3, t + 5, o)
                if has(3):
                    wait(dve, "xn_ready", 2 * T + t + 4)
                    wait(dve, "sc_v", 2 * (t + 3))
                    dve.tensor_reduce(sc_m[:, 0:1], xn[:, o, :], AX.X, ALU.max, apply_absolute_value=True)\
                        .then_inc(s["x_max"], 1)
                if has(5):
                    ln_mean_ready(dve, 3, t + 5)
                if has(-1):
                    wait(dve, "silu_done", t)
                    dve.tensor_reduce(sc_m[:, 1:2], hact[:, o, :], AX.X, ALU.max, apply_absolute_value=True)\
                        .then_inc(s["h_max"], 1)
                if has(5):
                    ln_mean(dve, o)
                if has(0):
                    wait(dve, "conv_mm", t + 1)
                    wait(dve, "silu_done", t - 1)
                    dve.tensor_tensor(hpre[:, par, :], bank[par][:], f_cb[:], ALU.add).then_inc(s["hpre_done"], 1)
                if scales:
                    if has(-1):
                        wait(dve, "h_max", t)
                    else:
                        wait(dve, "x_max", t + 4)
                    dve.tensor_scalar(sc_c[:], sc_m[:], Q_EPS, None, ALU.max).then_inc(s["sc_v"], 1)
                if has(-3):
                    wait(dve, "x_out", t - 3)
                    dve.tensor_scalar(sc_l[:], sc_i[:, par, 1:2], 1.0, None, ALU.mult).then_inc(s["sc_late"], 1)
                if scales:
                    dve.wait_ge(s["sc_v"], 2 * (t + 3) + 1)
                    dve.reciprocal(sc_r[:], sc_c[:]).then_inc(s["sc_v"], 1)
                    if has(1):
                        wait(dve, "xq_ready", t + 2)
                    if has(-3):
                        wait(dve, "sc_late", t - 2)
                    dve.tensor_tensor(sc_i[:, par, :], sc_c[:], sc_f[:], ALU.mult)
                if scales:
                    dve.wait_ge(s["sc_v"], 2 * (t + 3) + 2)
                    if not has(-1) and has(1):
                        wait(dve, "q1_done", t + 2)
                    dve.tensor_scalar(sc_q[:, par, :], sc_r[:], 127.0, None, ALU.mult).then_inc(s["sc_ready"], 1)

            def ffn_start():
                dve.wait_ge(s["sc_set"], 3)
                lead_in(ffn, -5, -4)

            def ffn_weights_lower():
                for k in range(TAPS):
                    dve.wait_ge(s["tap_copied"], k + 1)
                    dve.tensor_tensor(f_wk_lo[:, k, :], bank[k][:], f_wk_hi[:, k, :], ALU.subtract)\
                        .then_inc(s["tap_split"], 1)
                lead_in(ffn, -1, -1)

            run_tiles(dve, attention1, 3, 2, lo=4, first=0, body=4, before={
                T - 2: ffn_start, T - 1: lambda: lead_in(ffn, -3, -3), T: lambda: lead_in(ffn, -2, -2),
                T + 1: ffn_weights_lower})
            run_tiles(dve, ffn, 5, 4, lo=4, first=0, body=4)

        @block.tensor
        def _(pe):
            def tr(dst, src):
                return pe.transpose(dst, src, ident)

            pe.wait_ge(s["const_in"], 16)

            def transpose_weights(L):
                pe.wait_ge(s["attn_w_in"], 16 * 8 * (L + 1))
                for n in range(4):
                    last = tr(bank[5 * L][:, n * P:(n + 1) * P], w_raw[:, L, n, :])
                last.then_inc(s["w_tr"], 1)

            transpose_weights(0)
            pe.wait_ge(s["w_copied"], 2)
            pe.wait_ge(s["ident16_done"], 1)
            pe.wait_ge(s["ones_set"], 4)

            def attention(L):
                def step(t, par, has):
                    n = L * T + t
                    o = 1 - par
                    if has(0):
                        wait(pe, "qk_ready", 2 * n + 2)
                        for half in range(2):
                            wait(pe, "sub_done", 2 * n + half - 1)
                            if L == 1:
                                pe.matmul(bank[half][:].rearrange("p (h k) -> p h k", k=S), ident16[:],
                                          neg_mask[:].unsqueeze(1).to_broadcast([P, 8, S]),
                                          start=True, stop=False, skip_group_check=True)
                            for rr in range(2):
                                r = half * 2 + rr
                                for b in range(BT):
                                    q = slice(b * S, (b + 1) * S)
                                    last = pe.matmul(bank[half][q, rr * 256:(rr + 1) * 256], qq[:, par, r, q],
                                                     kj[:, par, :, q], start=(L == 0), stop=True,
                                                     skip_group_check=True)
                            last.then_inc(s["scores_mm"], 1)
                    if has(1):
                        wait(pe, "xn_ready", L * T + t + 2)
                        wait(pe, "xc_copied", n + 1)
                        tr(bank[4][:, 0:P], xn[:, o, :])
                        pe.wait_ge(ctx_ld[o], L * T * 8 + (t + 1 + 1 + par) * 8)
                        tr(bank[4][:, P:2 * P], ctx_in[:, o, :]).then_inc(s["xc_tr"], 1)
                    if has(-2):
                        wait(pe, "o_norm", 2 * (n - 1))
                        wait(pe, "x_attn", n - 2)
                        tr(bank[7][:, 0:P], o_n[:, par, :]).then_inc(s["o_tr"], 1)
                    if has(-1):
                        for half in range(2):
                            wait(pe, "exp_done", 2 * (n - 1) + half + 1)
                            wait(pe, "p_copied", 2 * (n - 2) + half + 1)
                            for i in range(4):
                                c = (half * 4 + i) * P
                                last = tr(bank[2 + half][:, i * P:(i + 1) * P], prob[:, o, c:c + P])
                            last.then_inc(s["p_tr"], 1)
                    if has(1):
                        wait(pe, "xc_copied", n + 2)
                        wait(pe, "qk_ready", 2 * n + 2)
                        wait(pe, "v_ready", 2 * n + 2)
                        pe.matmul(bank[5][:, 0:P], w_t[:, L, 0, :], xct[:, o, 0, :, 0, :], start=True, stop=True)
                        pe.matmul(bank[5][:, P:2 * P], w_t[:, L, 1, :], xct[:, o, 1, :, 0, :], start=True, stop=True)
                        for b in range(BT):
                            keys = xct[:, o, 1, b, :, :].rearrange("p c k -> p (c k)")
                            last = pe.matmul(bank[5][:, (2 + b) * P:(3 + b) * P], keys, w_t[:, L, 2, :],
                                             start=True, stop=True)
                        last.then_inc(s["qkv_mm"], 1)
                    if has(-2):
                        wait(pe, "o_copied", n - 1)
                        pe.matmul(bank[7][:, P:2 * P], o_t[:], w_t[:, L, 3, :], start=True, stop=True)\
                            .then_inc(s["wo_mm"], 1)
                    if has(-1):
                        wait(pe, "p_copied", 2 * n)
                        wait(pe, "v_ready", 2 * n)
                        wait(pe, "o_norm", 2 * (n - 1))
                        for i in range(NPAIR):
                            w = BT * 2 * VW
                            last = pe.matmul(bank[6][:, i * w:(i + 1) * w], prob_t[:, i, :],
                                             vb[:, o, i, :, :, :].rearrange("p b h v -> p (b h v)"),
                                             start=True, stop=True)
                        last.then_inc(s["pv_mm"], 1)
                return step

            def experts(u, par, has):
                o = 1 - par

                def hidden(c):
                    k = EC * u + c - 4
                    if c == 0:
                        wait(pe, "mx_hi_done", u + 1)
                        wait(pe, "mx_lo_done", u + 1)
                    wait(pe, "relu_a" if c % 2 == 0 else "relu_v", EC // 2 * u + (c - 4) // 2 + 1)
                    hi, lo = mx_hi[:, par, :], mx_lo[:, par, :]
                    pe.matmul(bank[c % 4][:], ew1_hi[:, c, :], hi, start=True, stop=False)
                    pe.matmul(bank[c % 4][:], ew1_hi[:, c, :], lo, start=False, stop=False)
                    pe.matmul(bank[c % 4][:], ew1_lo[:, c, :], hi, start=False, stop=True).then_inc(s["hid_mm"], 1)

                if has(0):
                    for c in range(4):
                        hidden(c)
                if has(1):
                    wait(pe, "m_xn_ready", G * (u + 2))
                    wait(pe, "mx_copied", u + 1)
                    wait(pe, "mx_lo_done", u + 1)
                    for j in range(G):
                        last = tr(bank[4][:, j * P:(j + 1) * P], m_xn[:, j, :])
                    last.then_inc(s["mx_tr"], 1)
                if has(0):
                    for c in range(4, EC):
                        hidden(c)
                if has(1):
                    wait(pe, "mx_copied", u + 2)
                    wait(pe, "gate_v", GATE_STEPS * u + 1)
                    for j in range(G):
                        last = pe.matmul(bank[5][:, j * GW:(j + 1) * GW], mxt[:, j * P:(j + 1) * P], gate_w[:],
                                         start=True, stop=True)
                    last.then_inc(s["gate_mm"], 1)
                if has(0):
                    wait(pe, "relu_a", EC // 2 * (u + 1))
                    wait(pe, "relu_v", EC // 2 * (u + 1))
                    for j in range(G):
                        wait(pe, "y_v", E * (G * u + j - 1))
                        for e in range(E):
                            for c in range(2):
                                last = pe.matmul(bank[6 + j % 2][:, e * P:(e + 1) * P],
                                                 hid[:, 2 * e + c, j * P:(j + 1) * P], ew2[:, 2 * e + c, :],
                                                 start=(c == 0), stop=(c == 1))
                        last.then_inc(s["y_mm"], 1)

            def layer1_queries():
                pe.wait_ge(s["xc_copied"], T)
                pe.wait_ge(s["mask_v"], 4)
                pe.matmul(bank[4][:, 0:S], ones[0:S, :], m_diag[:], start=True, stop=True).then_inc(s["alive_mm"], 1)
                pe.wait_ge(s["setup_v"], 7)
                pe.wait_ge(s["ffn_sum"], 2)
                pe.matmul(bank[4][:, S:S + 2], ones, f_s[:, 0:2], start=True, stop=True).then_inc(s["sum_mm"], 1)

            def experts_lead():
                pe.wait_ge(s["v_ready"], 2 * T)
                pe.wait_ge(s["qk_ready"], 2 * T)
                transpose_weights(1)
                pe.wait_ge(s["tern"], 1)
                pe.wait_ge(s["w_copied"], 4)
                lead_in(experts, -1, -1, NG)

            def attention1_lead():
                pe.wait_ge(s["w_copied"], 4)
                pe.wait_ge(s["mx_copied"], NG)
                pe.wait_ge(s["mx_hi_done"], NG)
                pe.wait_ge(s["mx_lo_done"], NG)
                pe.wait_ge(s["gate_v"], GATE_STEPS * (NG - 1) + 1)
                lead_in(attention1, -1, -1)

            attention1 = attention(1)
            run_tiles(pe, attention(0), 3, 2, body=4, before={T - 1: layer1_queries, T: experts_lead})
            pe.wait_ge(s["x_attn"], T)
            pe.wait_ge(s["w_copied"], 4)
            pe.wait_ge(s["tern"], 1)
            pe.wait_ge(s["ew1_split"], 2)
            run_tiles(pe, experts, 2, 0, T=NG, first=0, before={NG - 1: attention1_lead})
            pe.wait_ge(s["y_v"], E * T)
            pe.wait_ge(s["mask_v"], 6)

            def ffn(t, par, has):
                o = 1 - par
                if has(0):
                    wait(pe, "xlo_copied", t + 1)
                    wait(pe, "hpre_done", t - 1)
                    for tap in range(TAPS):
                        hi = tap_hi[:, par, tap, :, :].rearrange("p b s -> p (b s)")
                        lo = tap_lo[:, par, tap, :, :].rearrange("p b s -> p (b s)")
                        pe.matmul(bank[par][:], hi, f_wk_hi[:, tap, :], start=(tap == 0), stop=False)
                        pe.matmul(bank[par][:], hi, f_wk_lo[:, tap, :], start=False, stop=False)
                        last = pe.matmul(bank[par][:], lo, f_wk_hi[:, tap, :], start=False, stop=(tap == TAPS - 1))
                    last.then_inc(s["conv_mm"], 1)
                if has(-3):
                    wait(pe, "q2_copied", t - 2)
                    wait(pe, "x_out", t - 3)
                    for c in range(FC):
                        last = pe.matmul(bank[6][:, 0:P], q2t[:, o, c * P:(c + 1) * P], f_w2t[:, c, :],
                                         start=(c == 0), stop=(c == FC - 1))
                    last.then_inc(s["out_mm"], 1)
                if has(2):
                    wait(pe, "xq_ready", t + 3)
                    tr(bank[4][:, 0:P], xdq[:, par, :]).then_inc(s["xq_tr"], 1)
                if has(-2):
                    wait(pe, "q2_ready", t - 1)
                    if not has(-3):
                        wait(pe, "q2_copied", t - 2)
                    for c in range(FC):
                        last = tr(bank[5][:, c * P:(c + 1) * P], q2[:, par, c * P:(c + 1) * P])
                    last.then_inc(s["q2_tr"], 1)

            def ffn_weights():
                pe.wait_ge(s["sub_done"], 4 * T)
                pe.wait_ge(s["p_copied"], 4 * T)
                for tap in range(TAPS):
                    pe.wait_ge(s["tap_ready"], FC * (tap + 1))
                    for c in range(FC):
                        last = tr(bank[tap][:, c * P:(c + 1) * P], f_tap[:, tap, c, :])
                    last.then_inc(s["tap_tr"], 1)
                for c in range(FC):
                    last = tr(bank[3][:, c * P:(c + 1) * P], f_w2[:, c * P:(c + 1) * P])
                last.then_inc(s["tap_tr"], 1)
                lead_in(ffn, -1, -1)

            def ffn_lead():
                pe.wait_ge(s["xc_copied"], 2 * T)
                lead_in(ffn, -2, -2)

            run_tiles(pe, attention1, 3, 2, first=0, body=4, before={T: ffn_lead, T + 1: ffn_weights})
            pe.wait_ge(s["x_attn"], 2 * T)
            pe.wait_ge(s["tap_copied"], TAPS)
            pe.wait_ge(s["tap_split"], TAPS)
            pe.wait_ge(s["edges_set"], 4)
            pe.wait_ge(s["w2t_copied"], 1)
            run_tiles(pe, ffn, 5, 4, lo=4, first=0, body=4)


def constants(np):
    c = np.zeros((P, C_ALL), np.float32)
    p = np.arange(P)
    c[:, C_ID:C_ID + P] = np.eye(P)
    c[:, C_ONE:C_ONE + P] = 1
    for j in range(JH):
        c[:, C_J + j] = (p // HD) % JH == j
    for r in range(RQ):
        c[:, C_R + r] = p // (JH * HD) == r
    for h in range(2):
        c[:, C_H + h] = p // S == h
    for e in range(E):
        for f in range(E):
            c[:, C_TIE + e * E + f] = f < e
    for i, v in enumerate((0.75, 1.25, 1.75)):
        z = np.float32(math.log(math.expm1(v)))
        c[:, C_THR + i] = np.nextafter(z, np.float32(2)) if i == 1 else z
    c[:, C_POW] = -0.5
    c[:, C_RND] = ROUND
    c[:, C_EPS] = LN_EPS
    c[:, C_NEG] = -1
    return c


_INS = ['x', 'ctx_1024', 'mask_1x1xSxS2_ik0', 'g_xattn', 'g_ffn'] + [
    f"L{L}_xattn_{w}{c}" for L in range(2) for c in "qkvo" for w in "Wb"] + [
    f"L0_ffn_{n}" for n in ("gate_w", "gate_b", "dp_w1", "dp_b1", "dp_w2", "dp_b2", "ew1", "eb1", "ew2", "eb2")] + [
    f"L1_ffn_{n}" for n in ("w1", "conv_w", "conv_b", "w2")]


def kernel(**inputs):
    import numpy as np
    import concourse.bacc as bacc
    from concourse.bass_utils import run_bass_kernel_spmd

    nc = bacc.Bacc("TRN2", target_bir_lowering=False, num_devices=1)
    arrays, aps = {}, {}
    for name in _INS:
        v = np.ascontiguousarray(inputs[name])
        arrays[f"in_{name}"] = v
        aps[name] = nc.dram_tensor(f"in_{name}", v.shape, mybir.dt.from_np(v.dtype), kind="ExternalInput").ap()
    arrays["in_const"] = constants(np)
    aps["const"] = nc.dram_tensor("in_const", (P, C_ALL), F32, kind="ExternalInput").ap()
    out = nc.dram_tensor("out_x", (B, S, D), F32, kind="ExternalOutput").ap()
    build(nc, aps, out)
    r = run_bass_kernel_spmd(nc, [arrays], core_ids=[0])
    return r.results[0]["out_x"]
```
